# Optimizing a Trainium2 kernel written in Bass

```python
import numpy as np
import jax
import jax.numpy as jnp

def _softmax(x, axis=-1):
    return jax.nn.softmax(x, axis=axis)

def _gelu(x):
    return jax.nn.gelu(x, approximate=True)

def _silu(x):
    return jax.nn.silu(x)

def _sigmoid(x):
    return jax.nn.sigmoid(x)

def _layernorm(x, axis=-1, eps=1e-05):
    m = jnp.mean(x, axis=axis, keepdims=True)
    v = jnp.var(x, axis=axis, keepdims=True)
    return (x - m) / jnp.sqrt(v + eps)

def _scatter_add(tgt, idx, src, axis=0):
    return tgt.at[idx].add(src)

def _segment_sum(src, seg, n):
    return jax.ops.segment_sum(src, seg, n)
kernel_name = 'mk_adj_ffn_d1_adj_r2_adeead'

def setup_inputs(seed: int=0):
    np.random.seed(seed)
    _w = jnp.asarray

    def _rec_inputs():
        import jax
        import jax.numpy as jnp
        _gk = jax.random.key(seed)
        x = -0.000929 + 1 * jax.random.normal(jax.random.fold_in(_gk, 1), (3327, 128), jnp.float32)
        _w = (1.0 + jnp.arange(3327, dtype=jnp.float32)) ** (-0.5)
        _w = _w / _w.mean()
        _pij = jnp.clip(0.00240457 * _w[:, None] * _w[None, :], 0.0, 1.0)
        _a = jax.random.uniform(jax.random.fold_in(_gk, 2), (3327, 3327)) < _pij
        _a = jnp.logical_or(_a, jnp.eye(3327, dtype=bool))
        _af = _a.astype(jnp.float32)
        adj = _af
        return (x, adj)
    x, adj = _rec_inputs()

    def _L0_gnn_setup():
        import jax, jax.numpy as jnp
        import numpy as np
        ALPHA = 0.2
        NEG_INF = -9000000000000000.0
        LN_EPS = 1e-05
        N = 2048
        IN_F = 128
        OUT_F = 128
        HEADS = 4
        HEAD_DIM = OUT_F // HEADS
        EDGE_PROB = 0.02
        key = jax.random.key(seed)
        kx, ka, kw, kav = jax.random.split(key, 4)
        x = jax.random.normal(kx, (N, IN_F), dtype=jnp.float32)
        adj = jax.random.bernoulli(ka, EDGE_PROB, (N, N)).astype(jnp.float32)
        adj = jnp.maximum(adj, jnp.eye(N, dtype=jnp.float32))

        def xavier(k, shape, gain=1.414):
            fan_in, fan_out = (shape[0], shape[1])
            bound = gain * np.sqrt(6.0 / (fan_in + fan_out))
            return jax.random.uniform(k, shape, jnp.float32, -bound, bound)
        W = xavier(kw, (IN_F, OUT_F))
        a = xavier(kav, (2 * HEAD_DIM, 1))
        gamma = jnp.ones((OUT_F,), dtype=jnp.float32)
        beta = jnp.zeros((OUT_F,), dtype=jnp.float32)
        return {'x': x, 'adj': adj, 'W': W, 'a': a, 'gamma': gamma, 'beta': beta}
    _L0_gnn_all = _L0_gnn_setup()
    _L0_gnn_in = {k: v for k, v in _L0_gnn_all.items() if k in ('W', 'a', 'gamma', 'beta')}
    del _L0_gnn_all

    def _L0_ffn_setup():
        import jax, jax.numpy as jnp
        import numpy as np
        DIM = 128
        HEADS = 8
        NUM_KEYS = 128
        NUM_KV = NUM_KEYS ** 2
        PK_TOPK = 16
        FINAL_TOPK = 16
        DIM_KEY = DIM // 2
        P = 2

        def _pk(x, Wq_pk, pk_keys):
            b, n, _ = x.shape
            q = (x @ Wq_pk).reshape(b, n, P, HEADS, DIM_KEY).transpose(2, 0, 1, 3, 4)
            sim = jnp.einsum('pbnhd,pkhd->pbnhk', q, pk_keys)
            scores, idx = jax.lax.top_k(sim, PK_TOPK)
            idx0 = idx[0]
            idx1 = idx[1] * NUM_KEYS
            index = (idx0[..., :, None] + idx1[..., None, :]).reshape(b, n, HEADS, PK_TOPK * PK_TOPK)
            score = (scores[0][..., :, None] + scores[1][..., None, :]).reshape(b, n, HEADS, PK_TOPK * PK_TOPK)
            final_scores, pk_idx = jax.lax.top_k(score, FINAL_TOPK)
            final_indices = jnp.take_along_axis(index, pk_idx, axis=-1)
            final_scores = jax.nn.softmax(final_scores, axis=-1)
            return (final_scores, final_indices)
        key = jax.random.key(seed)
        ks = jax.random.split(key, 7)
        b, n = (2, 512)
        std = 0.02
        x = jax.random.normal(ks[0], (b, n, DIM), dtype=jnp.float32)
        Wq_pk = jax.random.normal(ks[1], (DIM, P * HEADS * DIM_KEY), dtype=jnp.float32) * std
        pk_keys = jax.random.normal(ks[2], (P, NUM_KEYS, HEADS, DIM_KEY), dtype=jnp.float32) * std
        Wq = jax.random.normal(ks[3], (DIM, HEADS * DIM), dtype=jnp.float32) * std
        keys_table = jax.random.normal(ks[4], (NUM_KV * HEADS, DIM), dtype=jnp.float32) * std
        values_table = jax.random.normal(ks[5], (NUM_KV * HEADS, DIM), dtype=jnp.float32) * std
        Wo = jax.random.normal(ks[6], (DIM * HEADS, DIM), dtype=jnp.float32) * std
        return {'x': x, 'Wq_pk': Wq_pk, 'pk_keys': pk_keys, 'Wq': Wq, 'keys_table': keys_table, 'values_table': values_table, 'Wo': Wo}
    _L0_ffn_all = _L0_ffn_setup()
    _L0_ffn_in = {k: v for k, v in _L0_ffn_all.items() if k in ('Wq_pk', 'pk_keys', 'Wq', 'keys_table', 'values_table', 'Wo')}
    del _L0_ffn_all
    return {'x': x, 'adj': adj, 'L0_gnn_W': _L0_gnn_in['W'], 'L0_gnn_a': _L0_gnn_in['a'], 'L0_gnn_gamma': _L0_gnn_in['gamma'], 'L0_gnn_beta': _L0_gnn_in['beta'], 'L0_ffn_Wq_pk': _L0_ffn_in['Wq_pk'], 'L0_ffn_pk_keys': _L0_ffn_in['pk_keys'], 'L0_ffn_Wq': _L0_ffn_in['Wq'], 'L0_ffn_keys_table': _L0_ffn_in['keys_table'], 'L0_ffn_values_table': _L0_ffn_in['values_table'], 'L0_ffn_Wo': _L0_ffn_in['Wo']}

def reference(x, adj, L0_gnn_W, L0_gnn_a, L0_gnn_gamma, L0_gnn_beta, L0_ffn_Wq_pk, L0_ffn_pk_keys, L0_ffn_Wq, L0_ffn_keys_table, L0_ffn_values_table, L0_ffn_Wo):
    import jax
    import jax.numpy as jnp

    def _L0_gnn_ref(x, adj, W, a, gamma, beta):
        import jax, jax.numpy as jnp
        import numpy as np
        ALPHA = 0.2
        NEG_INF = -9000000000000000.0
        LN_EPS = 1e-05
        N = 2048
        IN_F = 128
        OUT_F = 128
        HEADS = 4
        HEAD_DIM = OUT_F // HEADS
        EDGE_PROB = 0.02
        n = x.shape[0]
        head_dim = a.shape[0] // 2
        heads = W.shape[1] // head_dim
        h = (x @ W).reshape(n, heads, head_dim)
        src = jnp.einsum('nhd,d->nh', h, a[:head_dim, 0])
        dst = jnp.einsum('nhd,d->nh', h, a[head_dim:, 0])
        e = src[:, :, None] + dst.T[None, :, :]
        e = jnp.where(e > 0, e, ALPHA * e)
        mask = adj[:, None, :] > 0
        e = jnp.where(mask, e, NEG_INF)
        attn = jax.nn.softmax(e, axis=-1)
        out = jnp.einsum('nhm,mhd->nhd', attn, h)
        out = out.reshape(n, heads * head_dim)
        mu = jnp.mean(out, axis=-1, keepdims=True)
        var = jnp.var(out, axis=-1, keepdims=True)
        out = (out - mu) / jnp.sqrt(var + LN_EPS) * gamma + beta
        return out

    def _L0_ffn_ref(x, Wq_pk, pk_keys, Wq, keys_table, values_table, Wo):
        import jax, jax.numpy as jnp
        import numpy as np
        DIM = 128
        HEADS = 8
        NUM_KEYS = 128
        NUM_KV = NUM_KEYS ** 2
        PK_TOPK = 16
        FINAL_TOPK = 16
        DIM_KEY = DIM // 2
        P = 2

        def _pk(x, Wq_pk, pk_keys):
            b, n, _ = x.shape
            q = (x @ Wq_pk).reshape(b, n, P, HEADS, DIM_KEY).transpose(2, 0, 1, 3, 4)
            sim = jnp.einsum('pbnhd,pkhd->pbnhk', q, pk_keys)
            scores, idx = jax.lax.top_k(sim, PK_TOPK)
            idx0 = idx[0]
            idx1 = idx[1] * NUM_KEYS
            index = (idx0[..., :, None] + idx1[..., None, :]).reshape(b, n, HEADS, PK_TOPK * PK_TOPK)
            score = (scores[0][..., :, None] + scores[1][..., None, :]).reshape(b, n, HEADS, PK_TOPK * PK_TOPK)
            final_scores, pk_idx = jax.lax.top_k(score, FINAL_TOPK)
            final_indices = jnp.take_along_axis(index, pk_idx, axis=-1)
            final_scores = jax.nn.softmax(final_scores, axis=-1)
            return (final_scores, final_indices)
        b, n, d = x.shape
        q = (x @ Wq).reshape(b, n, HEADS, DIM) * DIM ** (-0.5)
        kv_scores, indices = _pk(x, Wq_pk, pk_keys)
        offsets = jnp.arange(HEADS, dtype=indices.dtype) * NUM_KV
        ind = indices + offsets[None, None, :, None]
        k = jnp.einsum('bnhk,bnhkd->bnhd', kv_scores, keys_table[ind])
        v = jnp.einsum('bnhk,bnhkd->bnhd', kv_scores, values_table[ind])
        sim = jnp.einsum('bihd,bjhd->bhij', q, k)
        neg = -jnp.finfo(sim.dtype).max
        causal = jnp.tril(jnp.ones((n, n), dtype=bool))
        sim = jnp.where(causal, sim, neg)
        attn = jax.nn.softmax(sim, axis=-1)
        out = jnp.einsum('bhij,bjhd->bhid', attn, v)
        out = out.transpose(0, 2, 1, 3).reshape(b, n, HEADS * DIM)
        return out @ Wo
    x = x + _L0_gnn_ref(_layernorm(x, axis=-1), adj, L0_gnn_W, L0_gnn_a, L0_gnn_gamma, L0_gnn_beta)
    x = x + _L0_ffn_ref(_layernorm(x, axis=-1)[None], L0_ffn_Wq_pk, L0_ffn_pk_keys, L0_ffn_Wq, L0_ffn_keys_table, L0_ffn_values_table, L0_ffn_Wo)[0]
    return x

_drawn_inputs = setup_inputs


def setup_inputs(seed=0):
    import zlib

    import numpy as np

    out = dict(_drawn_inputs(seed))
    spreads = {'L0_gnn_gamma': (1.0, 0.2), 'L0_gnn_beta': (0.0, 0.1)}
    factors = {'L0_ffn_Wq_pk': 36.632,
     'L0_ffn_pk_keys': 35.25,
     'L0_ffn_Wq': 64.0,
     'L0_ffn_keys_table': 64.0,
     'L0_ffn_values_table': 35.471,
     'L0_ffn_Wo': 32.801}
    for name, (base, spread) in spreads.items():
        noise = np.random.default_rng([zlib.crc32(name.encode()), seed]).standard_normal(out[name].shape)
        drawn = base * np.exp(spread * noise) if base else spread * noise
        out[name] = jnp.asarray(drawn.astype(out[name].dtype))
    for name, factor in factors.items():
        out[name] = (out[name] * factor).astype(out[name].dtype)
    return out
```

```python
from contextlib import ExitStack

import concourse.bass as bass
from concourse import mybir

P = 128
ALU = mybir.AluOpType
ACT = mybir.ActivationFunctionType
AX_X = mybir.AxisListType.X
F32 = mybir.dt.float32
U32 = mybir.dt.uint32

LN_EPS = 1e-05
ALPHA = 0.2
NEG_INF = -9000000000000000.0
CAUSAL_NEG = -3.0e38
REMOVED = -3.4e38
TOPK = 16

RECTS = [(0, 1, 16), (1, 1, 8), (2, 2, 5), (4, 4, 3), (8, 8, 1)]
NCAND = sum(r * c for _, r, c in RECTS)


def build(nc, x, adj, gnn_w, a_src, a_dst, gamma, beta, wqpk_t, pk_t, wq, kv_table, wo, out):
    N = adj.shape[1]
    T = x.shape[1]
    NP = T * P
    GH = a_src.shape[1]
    HD = P // GH
    NH = wo.shape[1]
    NUM_KV = kv_table.shape[0] // NH
    NK = pk_t.shape[2]
    DK = pk_t.shape[0]
    CH = (T + 3) // 4
    SCALE = float(P) ** -0.5
    PAIRS = T // 2
    assert T % 2 == 0 and (T - 1) * P < N <= NP

    def width(b):
        return min(P, N - b * P)

    def chunk(c):
        return min(512, NP - c * 512)

    ACT_CHUNKS = [0, 1, 2, 3, 4, 5]
    DVE_CHUNKS = [c for c in range(CH) if c not in ACT_CHUNKS]

    chunks = [t // 4 + 1 for t in range(T)]
    chunk0 = [sum(chunks[:t]) for t in range(T)]
    CPH = sum(chunks)
    assert CPH % 2 == 0

    with ExitStack() as ctx:
        def sb(name, shape, dt=F32):
            return ctx.enter_context(nc.sbuf_tensor(name, shape, dt))

        def sem(name):
            return ctx.enter_context(nc.semaphore(name))

        ps = ctx.enter_context(nc.psum_tensor("ps", [P, 8, 512], F32))

        ident = sb("ident", [P, P])
        causal = sb("causal", [P, P])
        cand_no = sb("cand_no", [P, NCAND])
        head_base = sb("head_base", [P, NH])
        eps = sb("eps", [P, 1])
        w_sb = sb("w_sb", [P, P])
        asrc_sb = sb("asrc_sb", [P, GH])
        adst_sb = sb("adst_sb", [P, GH, P])
        gamma_sb = sb("gamma_sb", [P, P])
        beta_sb = sb("beta_sb", [P, P])
        wq_sb = sb("wq_sb", [P, NH, P])
        wo_sb = sb("wo_sb", [P, NH, P])
        wc_sb = sb("wc_sb", [P, 2 * NH, NK])
        wq_head = sb("wq_head", [P, P])
        xres = sb("xres", [P, T, P])
        xT = sb("xT", [P, NP])
        kT = sb("kT", [P, NP])
        v_sb = sb("v_sb", [P, T, P])
        big = sb("big", [P, 2 * NP + GH * NP + 4 * 512])
        h_sb = sb("h_sb", [P, T, P])
        z_sb = sb("z_sb", [P, 2, NP])
        s_sb = sb("s_sb", [P, T, GH])
        stat = sb("stat", [P, 4, T])
        cmax = sb("cmax", [P, 2])
        lmax = sb("lmax", [P, 2])
        negc = sb("negc", [P, 2])
        rsum = sb("rsum", [P, 2])
        rinv = sb("rinv", [P, 2])
        top_val = sb("top_val", [P, 2, 2, TOPK])
        top_idx = sb("top_idx", [P, 2, TOPK], U32)
        rest = sb("rest", [P, 2, NK])
        cand = sb("cand", [P, 2, NCAND])
        cand_rest = sb("cand_rest", [P, NCAND])
        fin_val = sb("fin_val", [P, TOPK])
        fin_pos = sb("fin_pos", [P, TOPK], U32)
        fin_neg = sb("fin_neg", [P, 1])
        hit = sb("hit", [P, TOPK, NCAND])
        row_f = sb("row_f", [P, TOPK])
        row_no = sb("row_no", [P, 2, TOPK], U32)
        wexp = sb("wexp", [P, TOPK])
        wsum = sb("wsum", [P, 1])
        wrec = sb("wrec", [P, 1])
        wts = sb("wts", [P, 2, TOPK])
        smax = sb("smax", [P, CH + 1])
        nmax = sb("nmax", [P, 1])
        rpart = sb("rpart", [P, CH])
        rtot = sb("rtot", [P, 1])
        rrec = sb("rrec", [P, 1])

        adj_sb = big[:, 0:2 * NP].rearrange("p (b n) -> p b n", b=2)
        d_bc = big[:, 2 * NP:(2 + GH) * NP].rearrange("p (h n) -> p h n", h=GH)
        gpt4 = big[:, (2 + GH) * NP:(2 + GH) * NP + 4 * 512].rearrange("p (b n) -> p b n", b=4)
        wqpk_sb = big[0:DK, 0:2 * NH * P].rearrange("p (h n) -> p h n", h=2 * NH)
        pk_sb = big[0:DK, NP:NP + 2 * NH * NK].rearrange("p (h n) -> p h n", h=2 * NH)
        rows_sb = big[:, 0:2 * TOPK * 256].rearrange("p (b k n) -> p b k n", b=2, k=TOPK)
        o1 = 2 * TOPK * 256
        diag = big[:, o1:o1 + TOPK * P].rearrange("p (k n) -> p k n", k=TOPK)
        o2 = o1 + TOPK * P
        pt_sb = big[:, o2:o2 + 1024].rearrange("p (b n) -> p b n", b=2)
        o3 = o2 + 1024
        k_tok = big[:, o3:o3 + P]
        qT = big[:, o3 + P:o3 + 2 * P]
        oT = big[:, o3 + 2 * P:o3 + 3 * P]
        prob = z_sb[:, 0, :]
        s_flat = s_sb[:, :, :].rearrange("p t h -> p (t h)")
        v_flat = v_sb[:, :, :].rearrange("p t n -> p (t n)")
        xres_flat = xres[:, :, :].rearrange("p t n -> p (t n)")
        wq_flat = wq_sb[:, :, :].rearrange("p h n -> p (h n)")
        wo_flat = wo_sb[:, :, :].rearrange("p h n -> p (h n)")
        wc_pairs = wc_sb[:, :, :].rearrange("p h n -> p (h n)")
        hb_flat = head_base[:, :]
        kT3 = kT[:, :].rearrange("p (t n) -> p t n", t=T)

        x_in = sem("x_in")
        weights_in = sem("weights_in")
        eps_set = sem("eps_set")
        consts = sem("consts")
        pool_own = sem("pool_own")
        dve_own = sem("dve_own")
        act_tick = sem("act_tick")
        var_ready = sem("var_ready")
        std_ready = sem("std_ready")
        xn_ready = sem("xn_ready")
        filled = sem("filled")
        emptied = [sem("emptied_act"), sem("emptied_dve")]
        adj_in = [sem("adj_in0"), sem("adj_in1")]
        adj_used = sem("adj_used")
        z_ready = sem("z_ready")
        negc_ready = sem("negc_ready")
        p_ready = sem("p_ready")
        gt_ps = sem("gt_ps")
        gt_act = sem("gt_act")
        gt_dve = sem("gt_dve")
        gnn_ps = sem("gnn_ps")
        gnn_read = sem("gnn_read")
        gnn_done = sem("gnn_done")
        x3_ready = sem("x3_ready")
        x3_ps = sem("x3_ps")
        x3T_act = sem("x3T_act")
        wq_ready = sem("wq_ready")
        scores_ready = sem("scores_ready")
        scores_read = sem("scores_read")
        fin_ready = sem("fin_ready")
        wexp_ready = sem("wexp_ready")
        rows_no_ready = sem("rows_no_ready")
        rows_in = [sem("rows_in0"), sem("rows_in1")]
        pool_tick = sem("pool_tick")
        dve_tick = sem("dve_tick")
        diag_ready = sem("diag_ready")
        kv_ps = sem("kv_ps")
        kv_staged = sem("kv_staged")
        kT_ps = sem("kT_ps")
        kT_ready = sem("kT_ready")
        q_ps = sem("q_ps")
        q_ready = sem("q_ready")
        s_ps = sem("s_ps")
        s_read = sem("s_read")
        nmax_ready = sem("nmax_ready")
        exp_done = sem("exp_done")
        pt_ps = sem("pt_ps")
        pt_ready = sem("pt_ready")
        o_ps = sem("o_ps")
        o_ready = sem("o_ready")
        y_ps = sem("y_ps")
        y_added = sem("y_added")
        out_done = sem("out_done")

        block = ctx.enter_context(nc.Block())

        B_SC, B_KV, B_S, B_T, B_O, B_M = 0, 1, 2, 4, 6, 7

        F_XT, F_H, F_HT = 0, CH, 2 * CH
        F_WC = 3 * CH
        F_S = F_WC + (2 * NH + 3) // 4
        F_D = F_S + 1
        F_END = F_D + GH * CH

        def prologue_fill(f):
            if f < F_H:
                c = f
                return xT[:, c * 512:c * 512 + chunk(c)], chunk(c)
            if f < F_HT:
                c = f - F_H
                return h_sb[:, 4 * c:4 * c + chunk(c) // P, :].rearrange("p t n -> p (t n)"), chunk(c)
            if f < F_WC:
                c = f - F_HT
                return kT[:, c * 512:c * 512 + chunk(c)], chunk(c)
            if f < F_S:
                c = f - F_WC
                return wc_sb[:, 4 * c:4 * c + 4, :].rearrange("p h n -> p (h n)"), 4 * NK
            if f < F_D:
                return s_sb[:, :, :].rearrange("p t h -> p (t h)"), T * GH
            hd, c = divmod(f - F_D, CH)
            return d_bc[:, hd, c * 512:c * 512 + chunk(c)], chunk(c)

        def need_emptied(eng, f):
            if f >= 1:
                eng.wait_ge(emptied[0], (f + 1) // 2)
            if f >= 2:
                eng.wait_ge(emptied[1], f // 2)

        @block.sync
        def _(sp):
            sp.dma_start(xres[:], x).then_inc(x_in, 16)
            for dst, src in ((w_sb[:], gnn_w), (asrc_sb[:], a_src), (adst_sb[:], a_dst), (gamma_sb[:], gamma),
                             (beta_sb[:], beta), (wqpk_sb, wqpk_t), (pk_sb, pk_t), (wq_sb[:], wq), (wo_sb[:], wo)):
                sp.dma_start(dst, src).then_inc(weights_in, 16)
            need_emptied(sp, F_S)
            for b in range(2):
                sp.dma_start(adj_sb[:, b, 0:N], adj[b * P:(b + 1) * P, :]).then_inc(adj_in[b], 16)
            with sp.Fori(1, PAIRS) as i:
                for b in range(2):
                    sp.wait_ge(adj_used, 2 * i + b - 1)
                    sp.dma_start(adj_sb[:, b, 0:N], adj[bass.ds(i * (2 * P) + b * P, P), :]).then_inc(adj_in[b], 16)
            sp.wait_ge(y_added, T * NH)
            sp.dma_start(out.rearrange("(t p) c -> p t c", p=P), xres[:]).then_inc(out_done, 16)
            sp.wait_ge(out_done, 16)

        @block.gpsimd
        def _(pool):
            nc.gpsimd.memset(ident[:], 0.0).then_inc(pool_own, 1)
            nc.gpsimd.memset(causal[:], 0.0).then_inc(pool_own, 1)
            pool.wait_ge(pool_own, 2)
            nc.gpsimd.affine_select(out=ident[:], in_=ident[:], compare_op=ALU.not_equal, fill=1.0, base=0,
                                    pattern=[[-1, P]], channel_multiplier=1).then_inc(consts, 1)
            nc.gpsimd.affine_select(out=causal[:], in_=causal[:], compare_op=ALU.is_ge, fill=CAUSAL_NEG, base=0,
                                    pattern=[[-1, P]], channel_multiplier=1).then_inc(consts, 1)
            nc.gpsimd.iota(cand_no[:], pattern=[[1, NCAND]], base=0, channel_multiplier=0,
                           allow_small_or_imprecise_dtypes=True).then_inc(consts, 1)
            nc.gpsimd.iota(head_base[:], pattern=[[NUM_KV // 2, NH]], base=0, channel_multiplier=0,
                           allow_small_or_imprecise_dtypes=True).then_inc(consts, 1)

            def gather(i, t):
                b = t % 2
                pool.wait_ge(rows_no_ready, i * T + t + 1)
                pool.sem_inc(pool_tick, 1)
                if not (t < 2 and isinstance(i, int) and i == 0):
                    pool.wait_ge(kv_ps, i * T + t - 1)
                    pool.sem_inc(pool_tick, 1)
                for k in range(TOPK):
                    nc.gpsimd.indirect_dma_start(rows_sb[:, b, k, :], None, kv_table[:, :],
                                                 bass.IndirectOffsetOnAxis(ap=row_no[:, b, k:k + 1], axis=0)
                                                 ).then_inc(rows_in[b], 16)

            for t in range(2):
                gather(0, t)

            def head(i, last):
                for t in range(2, T):
                    gather(i, t)
                if not last:
                    for t in range(2):
                        gather(i + 1, t)

            head(0, False)
            with pool.Fori(1, NH - 1) as i:
                head(i, False)
            head(NH - 1, True)

        @block.tensor
        def _(pe):
            def room(f):
                if f >= 8:
                    pe.wait_ge(emptied[f % 2], (f - 8) // 2 + 1)

            pe.wait_ge(consts, 4)
            pe.wait_ge(xn_ready, 1)
            for c in range(CH):
                f = F_XT + c
                room(f)
                for j in range(chunk(c) // P):
                    mm = pe.transpose(ps[:, f % 8, j * P:(j + 1) * P], v_sb[:, 4 * c + j, :], ident[:])
                mm.then_inc(filled, 1)
            pe.wait_ge(weights_in, 9 * 16)
            need_emptied(pe, F_H)
            for c in range(CH):
                f = F_H + c
                room(f)
                for j in range(chunk(c) // P):
                    t = 4 * c + j
                    mm = pe.matmul(ps[:, f % 8, j * P:(j + 1) * P], xT[:, t * P:(t + 1) * P], w_sb[:], start=True, stop=True)
                mm.then_inc(filled, 1)
            for c in range(CH):
                f = F_HT + c
                room(f)
                pe.matmul(ps[:, f % 8, 0:chunk(c)], w_sb[:], xT[:, c * 512:c * 512 + chunk(c)],
                          start=True, stop=True).then_inc(filled, 1)
            for c in range(2 * NH // 4):
                f = F_WC + c
                room(f)
                for j in range(4):
                    mm = pe.matmul(ps[:, f % 8, j * NK:(j + 1) * NK], wqpk_sb[:, 4 * c + j, :], pk_sb[:, 4 * c + j, :],
                                   start=True, stop=True)
                mm.then_inc(filled, 1)
            need_emptied(pe, F_WC)
            room(F_S)
            for t in range(T):
                mm = pe.matmul(ps[:, F_S % 8, t * GH:(t + 1) * GH], kT[:, t * P:(t + 1) * P], asrc_sb[:],
                               start=True, stop=True)
            mm.then_inc(filled, 1)
            for hd in range(GH):
                for c in range(CH):
                    f = F_D + hd * CH + c
                    room(f)
                    pe.matmul(ps[:, f % 8, 0:chunk(c)], adst_sb[:, hd, :], kT[:, c * 512:c * 512 + chunk(c)],
                              start=True, stop=True).then_inc(filled, 1)
            need_emptied(pe, F_END)

            def gnn_unit(it, u):
                n = it * 8 + u
                hd = u % GH
                b = u % 2

                def turn(c):
                    for j in range(chunk(c) // P):
                        m = 4 * c + j
                        w = width(m)
                        mm = pe.transpose(ps[0:w, c % 4, j * P:(j + 1) * P], z_sb[:, b, m * P:m * P + w], ident[:])
                    mm.then_inc(gt_ps, 1)

                def times_h(c):
                    if c in ACT_CHUNKS:
                        pe.wait_ge(gt_act, n * len(ACT_CHUNKS) + ACT_CHUNKS.index(c) + 1)
                    else:
                        pe.wait_ge(gt_dve, n * len(DVE_CHUNKS) + DVE_CHUNKS.index(c) + 1)
                    for j in range(chunk(c) // P):
                        m = 4 * c + j
                        w = width(m)
                        mm = pe.matmul(ps[:, 6 + b, 0:HD], gpt4[0:w, c % 4, j * P:(j + 1) * P],
                                       h_sb[0:w, m, hd * HD:(hd + 1) * HD], start=(m == 0), stop=(m == T - 1))
                    return mm

                pe.wait_ge(p_ready, n + 1)
                turn(0)
                turn(1)
                for c in range(CH):
                    if c == 0 and not (isinstance(it, int) and u < 2):
                        pe.wait_ge(gnn_read, n - 1)
                    mm = times_h(c)
                    if c + 2 < CH:
                        turn(c + 2)
                mm.then_inc(gnn_ps, 1)

            for u in range(8):
                gnn_unit(0, u)
            with pe.Fori(1, PAIRS) as it:
                for u in range(8):
                    gnn_unit(it, u)

            pe.wait_ge(x3_ready, 1)
            for c in range(CH):
                if c >= 2:
                    pe.wait_ge(x3T_act, c - 1)
                for j in range(chunk(c) // P):
                    mm = pe.transpose(ps[:, c % 2, j * P:(j + 1) * P], z_sb[:, 0, (4 * c + j) * P:(4 * c + j + 1) * P], ident[:])
                mm.then_inc(x3_ps, 1)
            pe.wait_ge(x3T_act, CH)

            def scores(i, t):
                if not (t == 0 and isinstance(i, int) and i == 0):
                    pe.wait_ge(scores_read, i * T + t)
                pe.matmul(ps[:, B_SC, 0:2 * NK], xT[:, t * P:(t + 1) * P],
                          wc_pairs[:, bass.ds(i * 2 * NK, 2 * NK)], start=True, stop=True).then_inc(scores_ready, 1)

            def attend(i, t, ahead):
                u = i * T + t
                if t == 0:
                    pe.wait_ge(wq_ready, i + 1)
                pe.matmul(ps[:, B_O, 0:P], wq_head[:], xT[:, t * P:(t + 1) * P], start=True, stop=True).then_inc(q_ps, 1)
                pe.wait_ge(diag_ready, u + 1)
                pe.wait_ge(rows_in[t % 2], (i * (T // 2) + t // 2 + 1) * (16 * TOPK))
                if not (t == 0 and isinstance(i, int) and i == 0):
                    pe.wait_ge(kv_staged, 2 * u)
                for k in range(TOPK):
                    mm = pe.matmul(ps[:, B_KV, 0:256], diag[:, k, :], rows_sb[:, t % 2, k, :],
                                   start=(k == 0), stop=(k == TOPK - 1))
                mm.then_inc(kv_ps, 1)
                if ahead is not None:
                    scores(*ahead)
                pe.wait_ge(kv_staged, 2 * u + 2)
                if not (t == 0 and isinstance(i, int) and i == 0):
                    pe.wait_ge(y_added, u)
                pe.transpose(ps[:, B_M, P:2 * P], k_tok, ident[:]).then_inc(kT_ps, 1)
                pe.wait_ge(q_ready, u + 1)
                pe.wait_ge(kT_ready, u + 1)
                for c in range(chunks[t]):
                    g = chunk0[t] + c
                    if not (g < 2 and isinstance(i, int) and i == 0):
                        pe.wait_ge(s_read, i * CPH + g - 1)
                    w = min(512, (t + 1) * P - c * 512)
                    pe.matmul(ps[:, B_S + g % 2, 0:w], qT, kT[:, c * 512:c * 512 + w], start=True, stop=True).then_inc(s_ps, 1)

                def turn(c):
                    pe.wait_ge(exp_done, i * CPH + chunk0[t] + c + 1)
                    w = min(4, t + 1 - 4 * c)
                    for j in range(w):
                        mm = pe.transpose(ps[:, B_T + (chunk0[t] + c) % 2, j * P:(j + 1) * P],
                                          prob[:, (4 * c + j) * P:(4 * c + j + 1) * P], ident[:])
                    mm.then_inc(pt_ps, 1)

                turn(0)
                for c in range(chunks[t]):
                    if c + 1 < chunks[t]:
                        turn(c + 1)
                    pe.wait_ge(pt_ready, i * CPH + chunk0[t] + c + 1)
                    for j in range(min(4, t + 1 - 4 * c)):
                        m = 4 * c + j
                        mm = pe.matmul(ps[:, B_O, 0:P], v_sb[:, m, :], pt_sb[:, (chunk0[t] + c) % 2, j * P:(j + 1) * P],
                                       start=(m == 0), stop=(m == t))
                mm.then_inc(o_ps, 1)
                pe.wait_ge(o_ready, u + 1)
                pe.matmul(ps[:, B_M, 2 * P:3 * P], oT, wo_flat[:, bass.ds(i * P, P)], start=True, stop=True).then_inc(y_ps, 1)

            for t in range(3):
                scores(0, t)

            def head(i, last):
                for t in range(T):
                    attend(i, t, (i, t + 3) if t + 3 < T else None if last else (i + 1, t + 3 - T))

            head(0, False)
            with pe.Fori(1, NH - 1) as i:
                head(i, False)
            head(NH - 1, True)

        @block.scalar
        def _(act):
            act.wait_ge(var_ready, 1)
            nc.scalar.activation(stat[:, 2, :], stat[:, 1, :], ACT.Sqrt, bias=eps[:], scale=1.0 / P).then_inc(std_ready, 1)
            for f in range(0, F_END, 2):
                dst, w = prologue_fill(f)
                act.wait_ge(filled, f + 1)
                nc.scalar.copy(dst, ps[:, f % 8, 0:w]).then_inc(emptied[0], 1)

            def softmax(it, u):
                n = it * 8 + u
                b = u % 2
                act.wait_ge(z_ready, n + 1)
                act.wait_ge(negc_ready, n + 1)
                nc.scalar.activation(z_sb[:, b, 0:N], z_sb[:, b, 0:N], ACT.Exp, bias=negc[:, b:b + 1],
                                     accum_out=rsum[:, b:b + 1]).then_inc(p_ready, 1)

            def copies(it, u):
                n = it * 8 + u
                for j, c in enumerate(ACT_CHUNKS):
                    act.wait_ge(gt_ps, n * CH + c + 1)
                    nc.scalar.copy(gpt4[:, c % 4, 0:chunk(c)], ps[:, c % 4, 0:chunk(c)]).then_inc(gt_act, 1)

            need_emptied(act, F_END)
            softmax(0, 0)
            for u in range(1, 8):
                softmax(0, u)
                copies(0, u - 1)
            with act.Fori(1, PAIRS) as it:
                for u in range(8):
                    softmax(it, u)
                    if u == 0:
                        copies(it - 1, 7)
                    else:
                        copies(it, u - 1)
            copies(PAIRS - 1, 7)

            for k in range(2):
                act.wait_ge(var_ready, 2 + k)
                nc.scalar.activation(stat[:, 2, :], stat[:, 1, :], ACT.Sqrt, bias=eps[:], scale=1.0 / P).then_inc(std_ready, 1)
            for c in range(CH):
                act.wait_ge(x3_ps, c + 1)
                nc.scalar.copy(xT[:, c * 512:c * 512 + chunk(c)], ps[:, c % 2, 0:chunk(c)]).then_inc(x3T_act, 1)

            def weights(i, t):
                act.wait_ge(fin_ready, i * T + t + 1)
                nc.scalar.activation(wexp[:], fin_val[:], ACT.Exp, bias=fin_neg[:], accum_out=wsum[:]).then_inc(wexp_ready, 1)

            def attend(i, t, ahead):
                u = i * T + t
                if t == 0:
                    if not (isinstance(i, int) and i == 0):
                        act.wait_ge(q_ps, u)
                        act.sem_inc(act_tick, 1)
                    nc.scalar.copy(wq_head[:], wq_flat[:, bass.ds(i * P, P)]).then_inc(wq_ready, 1)
                act.wait_ge(q_ps, u + 1)
                nc.scalar.copy(qT, ps[:, B_O, 0:P]).then_inc(q_ready, 1)
                if ahead is not None:
                    weights(*ahead)
                act.wait_ge(kv_ps, u + 1)
                nc.scalar.copy(k_tok, ps[:, B_KV, 0:P]).then_inc(kv_staged, 1)
                nc.scalar.copy(v_sb[:, t, :], ps[:, B_KV, P:2 * P]).then_inc(kv_staged, 1)
                act.wait_ge(nmax_ready, u + 1)
                for c in range(chunks[t] + 1):
                    if c < chunks[t]:
                        w = min(512, (t + 1) * P - c * 512)
                        nc.scalar.activation(prob[:, c * 512:c * 512 + w], prob[:, c * 512:c * 512 + w], ACT.Exp,
                                             bias=nmax[:], accum_out=rpart[:, c:c + 1]).then_inc(exp_done, 1)
                    if c >= 1:
                        g = chunk0[t] + c - 1
                        w = min(512, (t + 1) * P - (c - 1) * 512)
                        act.wait_ge(pt_ps, i * CPH + g + 1)
                        nc.scalar.copy(pt_sb[:, g % 2, 0:w], ps[:, B_T + g % 2, 0:w]).then_inc(pt_ready, 1)
                act.wait_ge(o_ps, u + 1)
                nc.scalar.copy(oT, ps[:, B_O, 0:P]).then_inc(o_ready, 1)

            weights(0, 0)
            weights(0, 1)

            def head(i, last):
                for t in range(T):
                    attend(i, t, (i, t + 2) if t + 2 < T else None if last else (i + 1, t + 2 - T))

            head(0, False)
            with act.Fori(1, NH - 1) as i:
                head(i, False)
            head(NH - 1, True)

        @block.vector
        def _(dve):
            own = [0]

            def mark(ins):
                own[0] += 1
                ins.then_inc(dve_own, 1)
                return own[0]

            def after(n):
                dve.wait_ge(dve_own, n)

            def restart():
                after(own[0])
                dve.sem_clear(dve_own)
                own[0] = 0

            def bc(ap):
                return ap.unsqueeze(2).to_broadcast([P, T, P])

            def norm(dst, src, k):
                after(mark(nc.vector.tensor_reduce(stat[:, 0, :], src, AX_X, ALU.add)))
                after(mark(nc.vector.tensor_scalar(stat[:, 0, :], stat[:, 0, :], 1.0 / P, None, ALU.mult)))
                after(mark(nc.vector.tensor_tensor(dst, src, bc(stat[:, 0, :]), ALU.subtract)))
                after(mark(nc.vector.tensor_tensor(kT3, dst, dst, ALU.mult)))
                nc.vector.tensor_reduce(stat[:, 1, :], kT3, AX_X, ALU.add).then_inc(var_ready, 1)
                dve.wait_ge(std_ready, k)
                after(mark(nc.vector.reciprocal(stat[:, 3, :], stat[:, 2, :])))
                return nc.vector.tensor_tensor(dst, dst, bc(stat[:, 3, :]), ALU.mult)

            after(mark(nc.vector.memset(eps[:], LN_EPS)))
            dve.wait_ge(x_in, 16)
            norm(v_sb[:], xres[:], 1).then_inc(xn_ready, 1)
            for f in range(1, F_END, 2):
                dst, w = prologue_fill(f)
                dve.wait_ge(filled, f + 1)
                nc.vector.tensor_copy(dst, ps[:, f % 8, 0:w]).then_inc(emptied[1], 1)
            dve.wait_ge(consts, 4)
            after(mark(nc.vector.tensor_scalar(head_base[:], head_base[:], 2.0, None, ALU.mult)))
            need_emptied(dve, F_END)
            restart()

            def mask_row(it, u):
                tt = u // GH
                dve.wait_ge(adj_in[tt], it * 16 + 16)
                return mark(nc.vector.tensor_scalar(adj_sb[:, tt, 0:N], adj_sb[:, tt, 0:N], 0.0, NEG_INF,
                                                    ALU.is_le, ALU.mult))

            def logits(it, u):
                n = it * 8 + u
                hd, b, tt = u % GH, u % 2, u // GH
                if hd == 0:
                    m = mask_row(it, u)
                else:
                    m = 0
                if not (isinstance(it, int) and u < 2):
                    dve.wait_ge(gnn_ps, n - 1)
                dve.sem_inc(dve_tick, 1)
                if m:
                    after(m)
                z = z_sb[:, b, 0:N]
                after(mark(nc.vector.tensor_scalar(z, adj_sb[:, tt, 0:N], s_flat[:, bass.ds(n, 1)], None, ALU.add)))
                after(mark(nc.vector.tensor_tensor_reduce(out=z, in0=d_bc[:, hd, 0:N], in1=z, scale=1.0, scalar=-3.4e38,
                                                          op0=ALU.add, op1=ALU.max, accum_out=cmax[:, b:b + 1])))
                nc.vector.scalar_tensor_tensor(out=z, in0=z, scalar=ALPHA, in1=z, op0=ALU.mult,
                                               op1=ALU.max).then_inc(z_ready, 1)
                after(mark(nc.vector.scalar_tensor_tensor(out=lmax[:, b:b + 1], in0=cmax[:, b:b + 1], scalar=ALPHA,
                                                          in1=cmax[:, b:b + 1], op0=ALU.mult, op1=ALU.max)))
                nc.vector.tensor_scalar(negc[:, b:b + 1], lmax[:, b:b + 1], -1.0, None, ALU.mult).then_inc(negc_ready, 1)
                if hd == GH - 1:
                    dve.sem_inc(adj_used, 1)

            def collect(it, u):
                n = it * 8 + u
                hd, b, tt = u % GH, u % 2, u // GH
                for c in DVE_CHUNKS:
                    dve.wait_ge(gt_ps, n * CH + c + 1)
                    nc.vector.tensor_copy(gpt4[:, c % 4, 0:chunk(c)], ps[:, c % 4, 0:chunk(c)]).then_inc(gt_dve, 1)
                dve.wait_ge(p_ready, n + 1)
                after(mark(nc.vector.reciprocal(rinv[:, b:b + 1], rsum[:, b:b + 1])))
                dve.wait_ge(gnn_ps, n + 1)
                nc.vector.tensor_scalar(v_flat[:, bass.ds(n * HD, HD)], ps[:, 6 + b, 0:HD], rinv[:, b:b + 1], None,
                                        ALU.mult).then_inc(gnn_read, 1)

            logits(0, 0)
            for u in range(1, 8):
                logits(0, u)
                collect(0, u - 1)
            restart()
            with dve.Fori(1, PAIRS) as it:
                for u in range(8):
                    logits(it, u)
                    if u == 0:
                        collect(it - 1, 7)
                    else:
                        collect(it, u - 1)
                dve.sem_inc(dve_tick, 1)
                restart()
            collect(PAIRS - 1, 7)
            dve.wait_ge(gnn_read, 4 * T)

            dve.wait_ge(weights_in, 9 * 16)
            after(mark(norm(v_sb[:], v_sb[:], 2)))
            g_bc = gamma_sb[:].unsqueeze(1).to_broadcast([P, T, P])
            b_bc = beta_sb[:].unsqueeze(1).to_broadcast([P, T, P])
            after(mark(nc.vector.tensor_tensor(v_sb[:], v_sb[:], g_bc, ALU.mult)))
            after(mark(nc.vector.tensor_tensor(v_sb[:], v_sb[:], b_bc, ALU.add)))
            after(mark(nc.vector.tensor_tensor(xres[:], xres[:], v_sb[:], ALU.add)))
            norm(z_sb[:, 0, :].rearrange("p (t n) -> p t n", t=T), xres[:], 3).then_inc(x3_ready, 1)
            restart()

            def top16(dst, idx, src, spare, first_done=None):
                a = mark(nc.vector.max(dst[:, 0:8], src))
                after(a)
                b = mark(nc.vector.max_index(idx[:, 0:8], dst[:, 0:8], src))
                c = mark(nc.vector.match_replace(spare, dst[:, 0:8], src, REMOVED))
                after(c)
                d = mark(nc.vector.max(dst[:, 8:16], spare))
                after(d)
                return mark(nc.vector.max_index(idx[:, 8:16], dst[:, 8:16], spare))

            def choose(i, t):
                u = i * T + t
                dve.wait_ge(scores_ready, u + 1)
                dve.sem_inc(dve_tick, 1)
                for half in range(2):
                    top16(top_val[:, half, 0, :], top_idx[:, half, :], ps[:, B_SC, half * NK:(half + 1) * NK], rest[:, half, :])
                after(own[0])
                dve.sem_inc(scores_read, 1)
                a = mark(nc.vector.tensor_scalar(top_val[:, 0, 1, :], top_idx[:, 0, :], hb_flat[:, bass.ds(i, 1)], None, ALU.add))
                b = mark(nc.vector.tensor_scalar(top_val[:, 1, 1, :], top_idx[:, 1, :], float(NK), None, ALU.mult))
                after(b)
                at = 0
                for i0, r, c in RECTS:
                    a0 = top_val[:, 0, :, i0:i0 + r].unsqueeze(3).to_broadcast([P, 2, r, c])
                    a1 = top_val[:, 1, :, 0:c].unsqueeze(2).to_broadcast([P, 2, r, c])
                    o = cand[:, :, at:at + r * c].rearrange("p k (r c) -> p k r c", r=r)
                    if r == 1:
                        a0 = top_val[:, 0, :, i0:i0 + 1].to_broadcast([P, 2, c])
                        a1 = top_val[:, 1, :, 0:c]
                        o = cand[:, :, at:at + c]
                    elif c == 1:
                        a0 = top_val[:, 0, :, i0:i0 + r]
                        a1 = top_val[:, 1, :, 0:1].to_broadcast([P, 2, r])
                        o = cand[:, :, at:at + r]
                    d = mark(nc.vector.tensor_tensor(o, a0, a1, ALU.add))
                    at += r * c
                after(d)
                if not (isinstance(i, int) and i == 0 and t == 0):
                    dve.wait_ge(wexp_ready, u)
                    dve.sem_inc(dve_tick, 1)
                top16(fin_val, fin_pos, cand[:, 0, :], cand_rest[:])
                after(own[0])
                nc.vector.tensor_scalar(fin_neg[:], fin_val[:, 0:1], -1.0, None, ALU.mult).then_inc(fin_ready, 1)
                after(mark(nc.vector.tensor_tensor(hit[:], fin_pos[:].unsqueeze(2).to_broadcast([P, TOPK, NCAND]),
                                                   cand_no[:].unsqueeze(1).to_broadcast([P, TOPK, NCAND]), ALU.is_equal)))
                after(mark(nc.vector.tensor_tensor(hit[:], hit[:], cand[:, 1, :].unsqueeze(1).to_broadcast([P, TOPK, NCAND]),
                                                   ALU.mult)))
                after(mark(nc.vector.tensor_reduce(row_f[:], hit[:], AX_X, ALU.add)))
                if not (isinstance(i, int) and i == 0 and t < 2):
                    dve.wait_ge(rows_in[t % 2], (i * (T // 2) + t // 2) * (16 * TOPK))
                nc.vector.tensor_copy(row_no[:, t % 2, :], row_f[:]).then_inc(rows_no_ready, 1)
                dve.wait_ge(wexp_ready, u + 1)
                after(mark(nc.vector.reciprocal(wrec[:], wsum[:])))
                after(mark(nc.vector.tensor_scalar(wts[:, t % 2, :], wexp[:], wrec[:, 0:1], None, ALU.mult)))
                restart()

            def spread(i, t):
                u = i * T + t
                if not (isinstance(i, int) and i == 0 and t == 0):
                    dve.wait_ge(kv_ps, u)
                nc.vector.tensor_tensor(diag, ident[:].unsqueeze(1).to_broadcast([P, TOPK, P]),
                                        wts[:, t % 2, :].unsqueeze(2).to_broadcast([P, TOPK, P]), ALU.mult).then_inc(diag_ready, 1)

            def attend(i, t, ahead, nxt):
                u = i * T + t
                if ahead is not None:
                    choose(*ahead)
                dve.wait_ge(kT_ps, u + 1)
                nc.vector.tensor_copy(kT[:, t * P:(t + 1) * P], ps[:, B_M, P:2 * P]).then_inc(kT_ready, 1)
                for c in range(chunks[t]):
                    g = chunk0[t] + c
                    w = min(512, (t + 1) * P - c * 512)
                    last = c == chunks[t] - 1
                    dve.wait_ge(s_ps, i * CPH + g + 1)
                    if last and w > P:
                        w -= P
                        mark(nc.vector.tensor_scalar(prob[:, c * 512:c * 512 + w], ps[:, B_S + g % 2, 0:w], SCALE, None,
                                                     ALU.mult, ALU.max, accum_out=smax[:, c:c + 1]))
                    elif not last:
                        nc.vector.tensor_scalar(prob[:, c * 512:c * 512 + w], ps[:, B_S + g % 2, 0:w], SCALE, None,
                                                ALU.mult, ALU.max, accum_out=smax[:, c:c + 1]).then_inc(s_read, 1)
                    else:
                        w = 0
                    if last:
                        k = c + (w > 0)
                        dve.sem_inc(dve_tick, 1)
                        nc.vector.tensor_tensor_reduce(
                            out=prob[:, t * P:(t + 1) * P], in0=ps[:, B_S + g % 2, w:w + P], in1=causal[:], scale=SCALE,
                            scalar=-3.4e38, op0=ALU.add, op1=ALU.max, accum_out=smax[:, k:k + 1]).then_inc(s_read, 1)
                dve.wait_ge(s_read, i * CPH + chunk0[t] + chunks[t])
                after(own[0]) if own[0] else None
                mark(nc.vector.tensor_reduce(rtot[:], smax[:, 0:k + 1], AX_X, ALU.max))
                after(own[0])
                nc.vector.tensor_scalar(nmax[:], rtot[:], -1.0, None, ALU.mult).then_inc(nmax_ready, 1)
                if nxt is not None:
                    spread(*nxt)
                dve.wait_ge(exp_done, i * CPH + chunk0[t] + chunks[t])
                after(mark(nc.vector.tensor_reduce(rtot[:], rpart[:, 0:chunks[t]], AX_X, ALU.add)))
                after(mark(nc.vector.reciprocal(rrec[:], rtot[:])))
                dve.wait_ge(y_ps, u + 1)
                row = xres_flat[:, t * P:(t + 1) * P]
                nc.vector.scalar_tensor_tensor(out=row, in0=ps[:, B_M, 2 * P:3 * P], scalar=rrec[:, 0:1], in1=row,
                                               op0=ALU.mult, op1=ALU.add).then_inc(y_added, 1)
                dve.wait_ge(y_added, u + 1)
                dve.sem_inc(dve_tick, 1)
                restart()

            choose(0, 0)
            choose(0, 1)
            spread(0, 0)

            def head(i, last):
                for t in range(T):
                    attend(i, t, (i, t + 2) if t + 2 < T else None if last else (i + 1, t + 2 - T),
                           (i, t + 1) if t + 1 < T else None if last else (i + 1, 0))

            head(0, False)
            with dve.Fori(1, NH - 1) as i:
                head(i, False)
            head(NH - 1, True)


def kernel(x, adj, L0_gnn_W, L0_gnn_a, L0_gnn_gamma, L0_gnn_beta, L0_ffn_Wq_pk, L0_ffn_pk_keys, L0_ffn_Wq,
           L0_ffn_keys_table, L0_ffn_values_table, L0_ffn_Wo):
    import numpy as np
    import concourse.bacc as bacc
    from concourse.bass_utils import run_bass_kernel_spmd

    n, d = np.shape(x)
    tiles = -(-n // P)
    xp = np.zeros((tiles * P, d), np.asarray(x).dtype)
    xp[:n] = x
    xp = np.ascontiguousarray(xp.reshape(tiles, P, d).transpose(1, 0, 2))
    adjp = np.zeros((tiles * P, n), np.asarray(adj).dtype)
    adjp[:n] = adj
    a = np.asarray(L0_gnn_a)[:, 0]
    hd = a.shape[0] // 2
    gh = d // hd
    a_src = np.zeros((d, gh), a.dtype)
    a_dst = np.zeros((d, gh, P), a.dtype)
    for h in range(gh):
        a_src[h * hd:(h + 1) * hd, h] = a[:hd]
        a_dst[h * hd:(h + 1) * hd, h, :] = a[hd:, None]
    gamma = np.ascontiguousarray(np.broadcast_to(np.asarray(L0_gnn_gamma)[None, :], (P, d)))
    beta = np.ascontiguousarray(np.broadcast_to(np.asarray(L0_gnn_beta)[None, :], (P, d)))
    pk = np.asarray(L0_ffn_pk_keys)
    halves, nk, nh, dk = pk.shape
    pk_t = np.ascontiguousarray(pk.transpose(3, 2, 0, 1)).reshape(dk, nh * halves, nk)
    wqpk = np.asarray(L0_ffn_Wq_pk).reshape(d, halves, nh, dk)
    wqpk_t = np.ascontiguousarray(wqpk.transpose(3, 2, 1, 0)).reshape(dk, nh * halves, d)
    wq = np.asarray(L0_ffn_Wq).reshape(d, nh, d)
    kv = np.concatenate([np.asarray(L0_ffn_keys_table), np.asarray(L0_ffn_values_table)], axis=1)
    wo = np.ascontiguousarray(np.asarray(L0_ffn_Wo).reshape(nh, d, d).transpose(1, 0, 2))

    nc = bacc.Bacc("TRN2", target_bir_lowering=False, num_devices=1)
    arrays = {"x_rows": xp, "adj_rows": adjp, "gnn_w": np.asarray(L0_gnn_W), "a_src": a_src, "a_dst": a_dst,
              "gamma": gamma, "beta": beta, "wqpk_t": wqpk_t, "pk_t": pk_t, "wq": wq, "kv_table": kv, "wo": wo}
    args = [nc.dram_tensor(name, v.shape, mybir.dt.from_np(v.dtype), kind="ExternalInput").ap()
            for name, v in arrays.items()]
    out = nc.dram_tensor("out_rows", (tiles * P, d), F32, kind="ExternalOutput").ap()
    build(nc, *args, out)
    r = run_bass_kernel_spmd(nc, [arrays], core_ids=[0])
    return r.results[0]["out_rows"][:n]
```

```python
from contextlib import ExitStack

import concourse.bass as bass
from concourse import mybir

P = 128
ALU = mybir.AluOpType
ACT = mybir.ActivationFunctionType
AX_X = mybir.AxisListType.X
F32 = mybir.dt.float32
U32 = mybir.dt.uint32

LN_EPS = 1e-05
ALPHA = 0.2
NEG_INF = -9000000000000000.0
CAUSAL_NEG = -3.0e38
REMOVED = -3.4e38
TOPK = 16

RECTS = [(0, 1, 16), (1, 1, 8), (2, 2, 5), (4, 4, 3), (8, 8, 1)]
NCAND = sum(r * c for _, r, c in RECTS)


def build(nc, x, adj, gnn_w, a_src, a_dst, gamma, beta, wqpk_t, pk_t, wq, kv_table, wo, out):
    N = adj.shape[1]
    T = x.shape[1]
    NP = T * P
    GH = a_src.shape[1]
    HD = P // GH
    NH = wo.shape[1]
    NUM_KV = kv_table.shape[0] // NH
    NK = pk_t.shape[2]
    DK = pk_t.shape[0]
    CH = (T + 3) // 4
    SCALE = float(P) ** -0.5
    PAIRS = T // 2
    assert T % 2 == 0 and (T - 1) * P < N <= NP

    def width(b):
        return min(P, N - b * P)

    def chunk(c):
        return min(512, NP - c * 512)

    ACT_CHUNKS = [0, 1, 2, 3, 4, 5]
    DVE_CHUNKS = [c for c in range(CH) if c not in ACT_CHUNKS]

    RR, RC = 3, 13
    AHEAD = 4

    def uses(r, b, t):
        return (t - b + r - 1) // r if t > b else 0

    def user_before(r, i, t):
        if t >= r:
            return i * T + t - r
        if isinstance(i, int) and i == 0:
            return None
        return (i - 1) * T + max(p for p in range(T) if p % r == t % r)

    chunks = [t // 4 + 1 for t in range(T)]
    chunk0 = [sum(chunks[:t]) for t in range(T)]
    CPH = sum(chunks)
    assert CPH % 2 == 0

    with ExitStack() as ctx:
        def sb(name, shape, dt=F32):
            return ctx.enter_context(nc.sbuf_tensor(name, shape, dt))

        def sem(name):
            return ctx.enter_context(nc.semaphore(name))

        ps = ctx.enter_context(nc.psum_tensor("ps", [P, 8, 512], F32))

        ident = sb("ident", [P, P])
        causal = sb("causal", [P, P])
        cand_no = sb("cand_no", [P, NCAND])
        head_base = sb("head_base", [P, NH])
        eps = sb("eps", [P, 1])
        w_sb = sb("w_sb", [P, P])
        asrc_sb = sb("asrc_sb", [P, GH])
        adst_sb = sb("adst_sb", [P, GH, P])
        gamma_sb = sb("gamma_sb", [P, P])
        beta_sb = sb("beta_sb", [P, P])
        wq_sb = sb("wq_sb", [P, NH, P])
        wo_sb = sb("wo_sb", [P, NH, P])
        wc_sb = sb("wc_sb", [P, 2 * NH, NK])
        wq_head = sb("wq_head", [P, P])
        xres = sb("xres", [P, T, P])
        xT = sb("xT", [P, NP])
        kT = sb("kT", [P, NP])
        v_sb = sb("v_sb", [P, T, P])
        big = sb("big", [P, 2 * NP + GH * NP + 4 * 512])
        h_sb = sb("h_sb", [P, T, P])
        z_sb = sb("z_sb", [P, 2, NP])
        s_sb = sb("s_sb", [P, T, GH])
        stat = sb("stat", [P, 4, T])
        cmax = sb("cmax", [P, 2])
        lmax = sb("lmax", [P, 2])
        negc = sb("negc", [P, 2])
        rsum = sb("rsum", [P, 2])
        rinv = sb("rinv", [P, 2])
        top_val = sb("top_val", [P, 2, 2, TOPK])
        top_idx = sb("top_idx", [P, 2, TOPK], U32)
        rest = sb("rest", [P, 2, NK])
        cand = sb("cand", [P, 2, NCAND])
        cand_rest = sb("cand_rest", [P, NCAND])
        fin_val = sb("fin_val", [P, RC, TOPK])
        fin_pos = sb("fin_pos", [P, TOPK], U32)
        fin_neg = sb("fin_neg", [P, RC])
        hit = sb("hit", [P, TOPK, NCAND])
        row_f = sb("row_f", [P, TOPK])
        row_no = sb("row_no", [P, RC, TOPK], U32)
        wexp = sb("wexp", [P, RC, TOPK])
        wsum = sb("wsum", [P, RC])
        wrec = sb("wrec", [P, 1])
        wts = sb("wts", [P, TOPK])
        smax = sb("smax", [P, CH + 1])
        nmax = sb("nmax", [P, 1])
        rpart = sb("rpart", [P, CH])
        rtot = sb("rtot", [P, 1])
        rrec = sb("rrec", [P, 1])

        adj_sb = big[:, 0:2 * NP].rearrange("p (b n) -> p b n", b=2)
        d_bc = big[:, 2 * NP:(2 + GH) * NP].rearrange("p (h n) -> p h n", h=GH)
        gpt4 = big[:, (2 + GH) * NP:(2 + GH) * NP + 4 * 512].rearrange("p (b n) -> p b n", b=4)
        wqpk_sb = big[0:DK, 0:2 * NH * P].rearrange("p (h n) -> p h n", h=2 * NH)
        pk_sb = big[0:DK, NP:NP + 2 * NH * NK].rearrange("p (h n) -> p h n", h=2 * NH)
        rows_sb = big[:, 0:RR * TOPK * 256].rearrange("p (b k n) -> p b k n", b=RR, k=TOPK)
        o1 = RR * TOPK * 256
        diag = big[:, o1:o1 + 2 * TOPK * P].rearrange("p (b k n) -> p b k n", b=2, k=TOPK)
        o2 = o1 + 2 * TOPK * P
        pt_sb = big[:, o2:o2 + 1024].rearrange("p (b n) -> p b n", b=2)
        o3 = o2 + 1024
        k_tok = big[:, o3:o3 + P]
        qT = big[:, o3 + P:o3 + 2 * P]
        oT = big[:, o3 + 2 * P:o3 + 3 * P]
        prob = z_sb[:, 0, :]
        s_flat = s_sb[:, :, :].rearrange("p t h -> p (t h)")
        v_flat = v_sb[:, :, :].rearrange("p t n -> p (t n)")
        xres_flat = xres[:, :, :].rearrange("p t n -> p (t n)")
        wq_flat = wq_sb[:, :, :].rearrange("p h n -> p (h n)")
        wo_flat = wo_sb[:, :, :].rearrange("p h n -> p (h n)")
        wc_pairs = wc_sb[:, :, :].rearrange("p h n -> p (h n)")
        hb_flat = head_base[:, :]
        kT3 = kT[:, :].rearrange("p (t n) -> p t n", t=T)

        x_in = sem("x_in")
        weights_in = sem("weights_in")
        eps_set = sem("eps_set")
        consts = sem("consts")
        pool_own = sem("pool_own")
        dve_own = sem("dve_own")
        act_tick = sem("act_tick")
        var_ready = sem("var_ready")
        std_ready = sem("std_ready")
        xn_ready = sem("xn_ready")
        filled = sem("filled")
        emptied = [sem("emptied_act"), sem("emptied_dve")]
        adj_in = [sem("adj_in0"), sem("adj_in1")]
        adj_used = sem("adj_used")
        z_ready = sem("z_ready")
        negc_ready = sem("negc_ready")
        p_ready = sem("p_ready")
        gt_ps = sem("gt_ps")
        gt_act = sem("gt_act")
        gt_dve = sem("gt_dve")
        gnn_ps = sem("gnn_ps")
        gnn_read = sem("gnn_read")
        gnn_done = sem("gnn_done")
        x3_ready = sem("x3_ready")
        x3_ps = sem("x3_ps")
        x3T_act = sem("x3T_act")
        wq_ready = sem("wq_ready")
        scores_ready = sem("scores_ready")
        scores_read = sem("scores_read")
        fin_ready = sem("fin_ready")
        wexp_ready = sem("wexp_ready")
        rows_no_ready = sem("rows_no_ready")
        rows_in = [sem(f"rows_in{b}") for b in range(RR)]
        pool_tick = sem("pool_tick")
        dve_tick = sem("dve_tick")
        diag_ready = sem("diag_ready")
        kv_ps = sem("kv_ps")
        kv_staged = sem("kv_staged")
        qk_ps = sem("qk_ps")
        qk_ready = sem("qk_ready")
        s_ps = sem("s_ps")
        s_read = sem("s_read")
        nmax_ready = sem("nmax_ready")
        exp_done = sem("exp_done")
        pt_ps = sem("pt_ps")
        pt_ready = sem("pt_ready")
        o_ps = sem("o_ps")
        o_ready = sem("o_ready")
        y_ps = sem("y_ps")
        y_added = sem("y_added")
        out_done = sem("out_done")

        block = ctx.enter_context(nc.Block())

        B_SC, B_KV, B_S, B_T, B_O, B_M = 0, 1, 2, 4, 6, 7

        F_XT, F_H, F_HT = 0, CH, 2 * CH
        F_WC = 3 * CH
        F_S = F_WC + (2 * NH + 3) // 4
        F_D = F_S + 1
        F_END = F_D + GH * CH

        def prologue_fill(f):
            if f < F_H:
                c = f
                return xT[:, c * 512:c * 512 + chunk(c)], chunk(c)
            if f < F_HT:
                c = f - F_H
                return h_sb[:, 4 * c:4 * c + chunk(c) // P, :].rearrange("p t n -> p (t n)"), chunk(c)
            if f < F_WC:
                c = f - F_HT
                return kT[:, c * 512:c * 512 + chunk(c)], chunk(c)
            if f < F_S:
                c = f - F_WC
                return wc_sb[:, 4 * c:4 * c + 4, :].rearrange("p h n -> p (h n)"), 4 * NK
            if f < F_D:
                return s_sb[:, :, :].rearrange("p t h -> p (t h)"), T * GH
            hd, c = divmod(f - F_D, CH)
            return d_bc[:, hd, c * 512:c * 512 + chunk(c)], chunk(c)

        def need_emptied(eng, f):
            if f >= 1:
                eng.wait_ge(emptied[0], (f + 1) // 2)
            if f >= 2:
                eng.wait_ge(emptied[1], f // 2)

        @block.sync
        def _(sp):
            sp.dma_start(xres[:], x).then_inc(x_in, 16)
            for dst, src in ((w_sb[:], gnn_w), (asrc_sb[:], a_src), (adst_sb[:], a_dst), (gamma_sb[:], gamma),
                             (beta_sb[:], beta), (wqpk_sb, wqpk_t), (pk_sb, pk_t), (wq_sb[:], wq), (wo_sb[:], wo)):
                sp.dma_start(dst, src).then_inc(weights_in, 16)
            need_emptied(sp, F_S)
            for b in range(2):
                sp.dma_start(adj_sb[:, b, 0:N], adj[b * P:(b + 1) * P, :]).then_inc(adj_in[b], 16)
            with sp.Fori(1, PAIRS) as i:
                for b in range(2):
                    sp.wait_ge(adj_used, 2 * i + b - 1)
                    sp.dma_start(adj_sb[:, b, 0:N], adj[bass.ds(i * (2 * P) + b * P, P), :]).then_inc(adj_in[b], 16)
            sp.wait_ge(y_added, T * NH)
            sp.dma_start(out.rearrange("(t p) c -> p t c", p=P), xres[:]).then_inc(out_done, 16)
            sp.wait_ge(out_done, 16)

        @block.gpsimd
        def _(pool):
            nc.gpsimd.memset(ident[:], 0.0).then_inc(pool_own, 1)
            nc.gpsimd.memset(causal[:], 0.0).then_inc(pool_own, 1)
            pool.wait_ge(pool_own, 2)
            nc.gpsimd.affine_select(out=ident[:], in_=ident[:], compare_op=ALU.not_equal, fill=1.0, base=0,
                                    pattern=[[-1, P]], channel_multiplier=1).then_inc(consts, 1)
            nc.gpsimd.affine_select(out=causal[:], in_=causal[:], compare_op=ALU.is_ge, fill=CAUSAL_NEG, base=0,
                                    pattern=[[-1, P]], channel_multiplier=1).then_inc(consts, 1)
            nc.gpsimd.iota(cand_no[:], pattern=[[1, NCAND]], base=0, channel_multiplier=0,
                           allow_small_or_imprecise_dtypes=True).then_inc(consts, 1)
            nc.gpsimd.iota(head_base[:], pattern=[[NUM_KV // 2, NH]], base=0, channel_multiplier=0,
                           allow_small_or_imprecise_dtypes=True).then_inc(consts, 1)

            def gather(i, t):
                b = t % RR
                pool.wait_ge(rows_no_ready, i * T + t + 1)
                pool.sem_inc(pool_tick, 1)
                before = user_before(RR, i, t)
                if before is not None:
                    pool.wait_ge(kv_ps, before + 1)
                    pool.sem_inc(pool_tick, 1)
                for k in range(TOPK):
                    nc.gpsimd.indirect_dma_start(rows_sb[:, b, k, :], None, kv_table[:, :],
                                                 bass.IndirectOffsetOnAxis(ap=row_no[:, t % RC, k:k + 1], axis=0)
                                                 ).then_inc(rows_in[b], 16)

            for t in range(T):
                gather(0, t)
            with pool.Fori(1, NH) as i:
                for t in range(T):
                    gather(i, t)

        @block.tensor
        def _(pe):
            def room(f):
                if f >= 8:
                    pe.wait_ge(emptied[f % 2], (f - 8) // 2 + 1)

            pe.wait_ge(consts, 4)
            pe.wait_ge(xn_ready, 1)
            for c in range(CH):
                f = F_XT + c
                room(f)
                for j in range(chunk(c) // P):
                    mm = pe.transpose(ps[:, f % 8, j * P:(j + 1) * P], v_sb[:, 4 * c + j, :], ident[:])
                mm.then_inc(filled, 1)
            pe.wait_ge(weights_in, 9 * 16)
            need_emptied(pe, F_H)
            for c in range(CH):
                f = F_H + c
                room(f)
                for j in range(chunk(c) // P):
                    t = 4 * c + j
                    mm = pe.matmul(ps[:, f % 8, j * P:(j + 1) * P], xT[:, t * P:(t + 1) * P], w_sb[:], start=True, stop=True)
                mm.then_inc(filled, 1)
            for c in range(CH):
                f = F_HT + c
                room(f)
                pe.matmul(ps[:, f % 8, 0:chunk(c)], w_sb[:], xT[:, c * 512:c * 512 + chunk(c)],
                          start=True, stop=True).then_inc(filled, 1)
            for c in range(2 * NH // 4):
                f = F_WC + c
                room(f)
                for j in range(4):
                    mm = pe.matmul(ps[:, f % 8, j * NK:(j + 1) * NK], wqpk_sb[:, 4 * c + j, :], pk_sb[:, 4 * c + j, :],
                                   start=True, stop=True)
                mm.then_inc(filled, 1)
            need_emptied(pe, F_WC)
            room(F_S)
            for t in range(T):
                mm = pe.matmul(ps[:, F_S % 8, t * GH:(t + 1) * GH], kT[:, t * P:(t + 1) * P], asrc_sb[:],
                               start=True, stop=True)
            mm.then_inc(filled, 1)
            for hd in range(GH):
                for c in range(CH):
                    f = F_D + hd * CH + c
                    room(f)
                    pe.matmul(ps[:, f % 8, 0:chunk(c)], adst_sb[:, hd, :], kT[:, c * 512:c * 512 + chunk(c)],
                              start=True, stop=True).then_inc(filled, 1)
            need_emptied(pe, F_END)

            def gnn_unit(it, u):
                n = it * 8 + u
                hd = u % GH
                b = u % 2

                def turn(c):
                    for j in range(chunk(c) // P):
                        m = 4 * c + j
                        w = width(m)
                        mm = pe.transpose(ps[0:w, c % 4, j * P:(j + 1) * P], z_sb[:, b, m * P:m * P + w], ident[:])
                    mm.then_inc(gt_ps, 1)

                def times_h(c):
                    if c in ACT_CHUNKS:
                        pe.wait_ge(gt_act, n * len(ACT_CHUNKS) + ACT_CHUNKS.index(c) + 1)
                    else:
                        pe.wait_ge(gt_dve, n * len(DVE_CHUNKS) + DVE_CHUNKS.index(c) + 1)
                    for j in range(chunk(c) // P):
                        m = 4 * c + j
                        w = width(m)
                        mm = pe.matmul(ps[:, 6 + b, 0:HD], gpt4[0:w, c % 4, j * P:(j + 1) * P],
                                       h_sb[0:w, m, hd * HD:(hd + 1) * HD], start=(m == 0), stop=(m == T - 1))
                    return mm

                pe.wait_ge(p_ready, n + 1)
                turn(0)
                turn(1)
                for c in range(CH):
                    if c == 0 and not (isinstance(it, int) and u < 2):
                        pe.wait_ge(gnn_read, n - 1)
                    mm = times_h(c)
                    if c + 2 < CH:
                        turn(c + 2)
                mm.then_inc(gnn_ps, 1)

            for u in range(8):
                gnn_unit(0, u)
            with pe.Fori(1, PAIRS) as it:
                for u in range(8):
                    gnn_unit(it, u)

            pe.wait_ge(x3_ready, 1)
            for c in range(CH):
                if c >= 2:
                    pe.wait_ge(x3T_act, c - 1)
                for j in range(chunk(c) // P):
                    mm = pe.transpose(ps[:, c % 2, j * P:(j + 1) * P], z_sb[:, 0, (4 * c + j) * P:(4 * c + j + 1) * P], ident[:])
                mm.then_inc(x3_ps, 1)
            pe.wait_ge(x3T_act, CH)

            def scores(i, t):
                if not (t == 0 and isinstance(i, int) and i == 0):
                    pe.wait_ge(scores_read, i * T + t)
                pe.matmul(ps[:, B_SC, 0:2 * NK], xT[:, t * P:(t + 1) * P],
                          wc_pairs[:, bass.ds(i * 2 * NK, 2 * NK)], start=True, stop=True).then_inc(scores_ready, 1)

            def sum_rows(i, t):
                u = i * T + t
                pe.wait_ge(diag_ready, u + 1)
                pe.wait_ge(rows_in[t % RR], (i * uses(RR, t % RR, T) + t // RR + 1) * (16 * TOPK))
                if not (isinstance(i, int) and i == 0 and t == 0):
                    pe.wait_ge(kv_staged, 2 * u)
                for k in range(TOPK):
                    mm = pe.matmul(ps[:, B_KV, 0:256], diag[:, t % 2, k, :], rows_sb[:, t % RR, k, :],
                                   start=(k == 0), stop=(k == TOPK - 1))
                mm.then_inc(kv_ps, 1)

            def queries_keys(i, t):
                u = i * T + t
                if t == 0:
                    pe.wait_ge(wq_ready, i + 1)
                if not (isinstance(i, int) and i == 0 and t < 2):
                    pe.wait_ge(y_added, u - 1)
                elif t == 1:
                    pe.wait_ge(qk_ready, 2)
                pe.matmul(ps[:, B_M, 0:P], wq_head[:], xT[:, t * P:(t + 1) * P], start=True, stop=True)
                pe.wait_ge(kv_staged, 2 * u + 1)
                pe.transpose(ps[:, B_M, P:2 * P], k_tok, ident[:]).then_inc(qk_ps, 1)

            def out_part(i, t):
                pe.wait_ge(o_ready, i * T + t + 1)
                pe.matmul(ps[:, B_M, 2 * P:3 * P], oT, wo_flat[:, bass.ds(i * P, P)], start=True, stop=True).then_inc(y_ps, 1)

            def attend(i, t, before, nxt, ahead):
                u = i * T + t
                pe.wait_ge(qk_ready, 2 * u + 2)
                for c in range(chunks[t]):
                    g = chunk0[t] + c
                    if not (g < 2 and isinstance(i, int) and i == 0):
                        pe.wait_ge(s_read, i * CPH + g - 1)
                    w = min(512, (t + 1) * P - c * 512)
                    pe.matmul(ps[:, B_S + g % 2, 0:w], qT, kT[:, c * 512:c * 512 + w], start=True, stop=True).then_inc(s_ps, 1)
                    if c == 0 and before is not None:
                        out_part(*before)
                if ahead is not None:
                    scores(*ahead)
                if nxt is not None:
                    sum_rows(*nxt)
                    queries_keys(*nxt)

                def turn(c):
                    pe.wait_ge(exp_done, i * CPH + chunk0[t] + c + 1)
                    w = min(4, t + 1 - 4 * c)
                    for j in range(w):
                        mm = pe.transpose(ps[:, B_T + (chunk0[t] + c) % 2, j * P:(j + 1) * P],
                                          prob[:, (4 * c + j) * P:(4 * c + j + 1) * P], ident[:])
                    mm.then_inc(pt_ps, 1)

                turn(0)
                pe.wait_ge(kv_staged, 2 * u + 2)
                for c in range(chunks[t]):
                    if c + 1 < chunks[t]:
                        turn(c + 1)
                    pe.wait_ge(pt_ready, i * CPH + chunk0[t] + c + 1)
                    for j in range(min(4, t + 1 - 4 * c)):
                        m = 4 * c + j
                        mm = pe.matmul(ps[:, B_O, 0:P], v_sb[:, m, :], pt_sb[:, (chunk0[t] + c) % 2, j * P:(j + 1) * P],
                                       start=(m == 0), stop=(m == t))
                mm.then_inc(o_ps, 1)

            def step(i, t, d):
                if t + d < T:
                    return (i, t + d)
                return None if isinstance(i, int) and i == NH - 1 else (i + 1, t + d - T)

            for t in range(AHEAD):
                scores(0, t)
            sum_rows(0, 0)
            queries_keys(0, 0)

            def head(i):
                for t in range(T):
                    before = (i, t - 1) if t else None if isinstance(i, int) and i == 0 else (i - 1, T - 1)
                    attend(i, t, before, step(i, t, 1), step(i, t, AHEAD))

            head(0)
            with pe.Fori(1, NH - 1) as i:
                head(i)
            head(NH - 1)
            pe.wait_ge(y_added, T * NH - 1)
            out_part(NH - 1, T - 1)

        @block.scalar
        def _(act):
            act.wait_ge(var_ready, 1)
            nc.scalar.activation(stat[:, 2, :], stat[:, 1, :], ACT.Sqrt, bias=eps[:], scale=1.0 / P).then_inc(std_ready, 1)
            for f in range(0, F_END, 2):
                dst, w = prologue_fill(f)
                act.wait_ge(filled, f + 1)
                nc.scalar.copy(dst, ps[:, f % 8, 0:w]).then_inc(emptied[0], 1)

            def softmax(it, u):
                n = it * 8 + u
                b = u % 2
                act.wait_ge(z_ready, n + 1)
                act.wait_ge(negc_ready, n + 1)
                nc.scalar.activation(z_sb[:, b, 0:N], z_sb[:, b, 0:N], ACT.Exp, bias=negc[:, b:b + 1],
                                     accum_out=rsum[:, b:b + 1]).then_inc(p_ready, 1)

            def copies(it, u):
                n = it * 8 + u
                for j, c in enumerate(ACT_CHUNKS):
                    act.wait_ge(gt_ps, n * CH + c + 1)
                    nc.scalar.copy(gpt4[:, c % 4, 0:chunk(c)], ps[:, c % 4, 0:chunk(c)]).then_inc(gt_act, 1)

            need_emptied(act, F_END)
            for u in range(8):
                softmax(0, u)
                copies(0, u)
            with act.Fori(1, PAIRS) as it:
                for u in range(8):
                    softmax(it, u)
                    copies(it, u)

            for k in range(2):
                act.wait_ge(var_ready, 2 + k)
                nc.scalar.activation(stat[:, 2, :], stat[:, 1, :], ACT.Sqrt, bias=eps[:], scale=1.0 / P).then_inc(std_ready, 1)
            for c in range(CH):
                act.wait_ge(x3_ps, c + 1)
                nc.scalar.copy(xT[:, c * 512:c * 512 + chunk(c)], ps[:, c % 2, 0:chunk(c)]).then_inc(x3T_act, 1)

            def weights(i, t):
                b = t % RC
                act.wait_ge(fin_ready, i * T + t + 1)
                nc.scalar.activation(wexp[:, b, :], fin_val[:, b, :], ACT.Exp, bias=fin_neg[:, b:b + 1],
                                     accum_out=wsum[:, b:b + 1]).then_inc(wexp_ready, 1)

            def values(i, t):
                nc.scalar.copy(v_sb[:, t, :], ps[:, B_KV, P:2 * P]).then_inc(kv_staged, 1)

            def keys_values(i, t):
                u = i * T + t
                if t == 0:
                    if not (isinstance(i, int) and i == 0):
                        act.wait_ge(qk_ps, u)
                        act.sem_inc(act_tick, 1)
                    nc.scalar.copy(wq_head[:], wq_flat[:, bass.ds(i * P, P)]).then_inc(wq_ready, 1)
                act.wait_ge(kv_ps, u + 1)
                nc.scalar.copy(k_tok, ps[:, B_KV, 0:P]).then_inc(kv_staged, 1)
                if t > 0 or (isinstance(i, int) and i == 0):
                    values(i, t)
                act.wait_ge(qk_ps, u + 1)
                nc.scalar.copy(qT, ps[:, B_M, 0:P]).then_inc(qk_ready, 1)
                nc.scalar.copy(kT[:, t * P:(t + 1) * P], ps[:, B_M, P:2 * P]).then_inc(qk_ready, 1)

            def attend(i, t, nxt, ahead):
                u = i * T + t
                act.wait_ge(nmax_ready, u + 1)
                for c in range(chunks[t]):
                    w = min(512, (t + 1) * P - c * 512)
                    nc.scalar.activation(prob[:, c * 512:c * 512 + w], prob[:, c * 512:c * 512 + w], ACT.Exp,
                                         bias=nmax[:], accum_out=rpart[:, c:c + 1]).then_inc(exp_done, 1)
                if nxt is not None:
                    keys_values(*nxt)
                for c in range(chunks[t]):
                    g = chunk0[t] + c
                    w = min(512, (t + 1) * P - c * 512)
                    act.wait_ge(pt_ps, i * CPH + g + 1)
                    nc.scalar.copy(pt_sb[:, g % 2, 0:w], ps[:, B_T + g % 2, 0:w]).then_inc(pt_ready, 1)
                act.wait_ge(o_ps, u + 1)
                nc.scalar.copy(oT, ps[:, B_O, 0:P]).then_inc(o_ready, 1)
                if t == T - 1 and nxt is not None:
                    values(*nxt)
                if ahead is not None:
                    weights(*ahead)

            def step(i, t, d):
                if t + d < T:
                    return (i, t + d)
                return None if isinstance(i, int) and i == NH - 1 else (i + 1, t + d - T)

            for t in range(AHEAD):
                weights(0, t)
            keys_values(0, 0)

            def head(i):
                for t in range(T):
                    attend(i, t, step(i, t, 1), step(i, t, AHEAD))

            head(0)
            with act.Fori(1, NH - 1) as i:
                head(i)
            head(NH - 1)

        @block.vector
        def _(dve):
            own = [0]

            def mark(ins):
                own[0] += 1
                ins.then_inc(dve_own, 1)
                return own[0]

            def after(n):
                dve.wait_ge(dve_own, n)

            def restart():
                after(own[0])
                dve.sem_clear(dve_own)
                own[0] = 0

            def bc(ap):
                return ap.unsqueeze(2).to_broadcast([P, T, P])

            def norm(dst, src, k):
                after(mark(nc.vector.tensor_reduce(stat[:, 0, :], src, AX_X, ALU.add)))
                after(mark(nc.vector.tensor_scalar(stat[:, 0, :], stat[:, 0, :], 1.0 / P, None, ALU.mult)))
                after(mark(nc.vector.tensor_tensor(dst, src, bc(stat[:, 0, :]), ALU.subtract)))
                after(mark(nc.vector.tensor_tensor(kT3, dst, dst, ALU.mult)))
                nc.vector.tensor_reduce(stat[:, 1, :], kT3, AX_X, ALU.add).then_inc(var_ready, 1)
                dve.wait_ge(std_ready, k)
                after(mark(nc.vector.reciprocal(stat[:, 3, :], stat[:, 2, :])))
                return nc.vector.tensor_tensor(dst, dst, bc(stat[:, 3, :]), ALU.mult)

            after(mark(nc.vector.memset(eps[:], LN_EPS)))
            dve.wait_ge(x_in, 16)
            norm(v_sb[:], xres[:], 1).then_inc(xn_ready, 1)
            for f in range(1, F_END, 2):
                dst, w = prologue_fill(f)
                dve.wait_ge(filled, f + 1)
                nc.vector.tensor_copy(dst, ps[:, f % 8, 0:w]).then_inc(emptied[1], 1)
            dve.wait_ge(consts, 4)
            after(mark(nc.vector.tensor_scalar(head_base[:], head_base[:], 2.0, None, ALU.mult)))
            need_emptied(dve, F_END)
            restart()

            def mask_row(it, u):
                tt = u // GH
                dve.wait_ge(adj_in[tt], it * 16 + 16)
                return mark(nc.vector.tensor_scalar(adj_sb[:, tt, 0:N], adj_sb[:, tt, 0:N], 0.0, NEG_INF,
                                                    ALU.is_le, ALU.mult))

            def logits(it, u):
                n = it * 8 + u
                hd, b, tt = u % GH, u % 2, u // GH
                if hd == 0:
                    m = mask_row(it, u)
                else:
                    m = 0
                if not (isinstance(it, int) and u < 2):
                    dve.wait_ge(gnn_ps, n - 1)
                dve.sem_inc(dve_tick, 1)
                if m:
                    after(m)
                z = z_sb[:, b, 0:N]
                after(mark(nc.vector.tensor_scalar(z, adj_sb[:, tt, 0:N], s_flat[:, bass.ds(n, 1)], None, ALU.add)))
                after(mark(nc.vector.tensor_tensor_reduce(out=z, in0=d_bc[:, hd, 0:N], in1=z, scale=1.0, scalar=-3.4e38,
                                                          op0=ALU.add, op1=ALU.max, accum_out=cmax[:, b:b + 1])))
                nc.vector.scalar_tensor_tensor(out=z, in0=z, scalar=ALPHA, in1=z, op0=ALU.mult,
                                               op1=ALU.max).then_inc(z_ready, 1)
                after(mark(nc.vector.scalar_tensor_tensor(out=lmax[:, b:b + 1], in0=cmax[:, b:b + 1], scalar=ALPHA,
                                                          in1=cmax[:, b:b + 1], op0=ALU.mult, op1=ALU.max)))
                nc.vector.tensor_scalar(negc[:, b:b + 1], lmax[:, b:b + 1], -1.0, None, ALU.mult).then_inc(negc_ready, 1)
                if hd == GH - 1:
                    dve.sem_inc(adj_used, 1)

            def collect(it, u):
                n = it * 8 + u
                hd, b, tt = u % GH, u % 2, u // GH
                for c in DVE_CHUNKS:
                    dve.wait_ge(gt_ps, n * CH + c + 1)
                    nc.vector.tensor_copy(gpt4[:, c % 4, 0:chunk(c)], ps[:, c % 4, 0:chunk(c)]).then_inc(gt_dve, 1)
                dve.wait_ge(p_ready, n + 1)
                after(mark(nc.vector.reciprocal(rinv[:, b:b + 1], rsum[:, b:b + 1])))
                dve.wait_ge(gnn_ps, n + 1)
                nc.vector.tensor_scalar(v_flat[:, bass.ds(n * HD, HD)], ps[:, 6 + b, 0:HD], rinv[:, b:b + 1], None,
                                        ALU.mult).then_inc(gnn_read, 1)

            logits(0, 0)
            for u in range(1, 8):
                logits(0, u)
                collect(0, u - 1)
            restart()
            with dve.Fori(1, PAIRS) as it:
                for u in range(8):
                    logits(it, u)
                    if u == 0:
                        collect(it - 1, 7)
                    else:
                        collect(it, u - 1)
                dve.sem_inc(dve_tick, 1)
                restart()
            collect(PAIRS - 1, 7)
            dve.wait_ge(gnn_read, 4 * T)

            dve.wait_ge(weights_in, 9 * 16)
            after(mark(norm(v_sb[:], v_sb[:], 2)))
            g_bc = gamma_sb[:].unsqueeze(1).to_broadcast([P, T, P])
            b_bc = beta_sb[:].unsqueeze(1).to_broadcast([P, T, P])
            after(mark(nc.vector.tensor_tensor(v_sb[:], v_sb[:], g_bc, ALU.mult)))
            after(mark(nc.vector.tensor_tensor(v_sb[:], v_sb[:], b_bc, ALU.add)))
            after(mark(nc.vector.tensor_tensor(xres[:], xres[:], v_sb[:], ALU.add)))
            norm(z_sb[:, 0, :].rearrange("p (t n) -> p t n", t=T), xres[:], 3).then_inc(x3_ready, 1)
            restart()

            def top16(dst, idx, src, spare, first_done=None):
                a = mark(nc.vector.max(dst[:, 0:8], src))
                after(a)
                b = mark(nc.vector.max_index(idx[:, 0:8], dst[:, 0:8], src))
                c = mark(nc.vector.match_replace(spare, dst[:, 0:8], src, REMOVED))
                after(c)
                d = mark(nc.vector.max(dst[:, 8:16], spare))
                after(d)
                return mark(nc.vector.max_index(idx[:, 8:16], dst[:, 8:16], spare))

            def choose(i, t):
                u = i * T + t
                dve.wait_ge(scores_ready, u + 1)
                dve.sem_inc(dve_tick, 1)
                for half in range(2):
                    top16(top_val[:, half, 0, :], top_idx[:, half, :], ps[:, B_SC, half * NK:(half + 1) * NK], rest[:, half, :])
                after(own[0])
                dve.sem_inc(scores_read, 1)
                a = mark(nc.vector.tensor_scalar(top_val[:, 0, 1, :], top_idx[:, 0, :], hb_flat[:, bass.ds(i, 1)], None, ALU.add))
                b = mark(nc.vector.tensor_scalar(top_val[:, 1, 1, :], top_idx[:, 1, :], float(NK), None, ALU.mult))
                after(b)
                at = 0
                for i0, r, c in RECTS:
                    a0 = top_val[:, 0, :, i0:i0 + r].unsqueeze(3).to_broadcast([P, 2, r, c])
                    a1 = top_val[:, 1, :, 0:c].unsqueeze(2).to_broadcast([P, 2, r, c])
                    o = cand[:, :, at:at + r * c].rearrange("p k (r c) -> p k r c", r=r)
                    if r == 1:
                        a0 = top_val[:, 0, :, i0:i0 + 1].to_broadcast([P, 2, c])
                        a1 = top_val[:, 1, :, 0:c]
                        o = cand[:, :, at:at + c]
                    elif c == 1:
                        a0 = top_val[:, 0, :, i0:i0 + r]
                        a1 = top_val[:, 1, :, 0:1].to_broadcast([P, 2, r])
                        o = cand[:, :, at:at + r]
                    d = mark(nc.vector.tensor_tensor(o, a0, a1, ALU.add))
                    at += r * c
                after(d)
                b = t % RC
                before = user_before(RC, i, t)
                if before is not None:
                    dve.wait_ge(wexp_ready, before + 1)
                    dve.sem_inc(dve_tick, 1)
                top16(fin_val[:, b, :], fin_pos, cand[:, 0, :], cand_rest[:])
                after(own[0])
                nc.vector.tensor_scalar(fin_neg[:, b:b + 1], fin_val[:, b, 0:1], -1.0, None, ALU.mult).then_inc(fin_ready, 1)
                after(mark(nc.vector.tensor_tensor(hit[:], fin_pos[:].unsqueeze(2).to_broadcast([P, TOPK, NCAND]),
                                                   cand_no[:].unsqueeze(1).to_broadcast([P, TOPK, NCAND]), ALU.is_equal)))
                after(mark(nc.vector.tensor_tensor(hit[:], hit[:], cand[:, 1, :].unsqueeze(1).to_broadcast([P, TOPK, NCAND]),
                                                   ALU.mult)))
                after(mark(nc.vector.tensor_reduce(row_f[:], hit[:], AX_X, ALU.add)))
                if before is not None:
                    bt = t - RC if t >= RC else max(p for p in range(T) if p % RC == t % RC)
                    bi = i if t >= RC else i - 1
                    dve.wait_ge(rows_in[bt % RR], (bi * uses(RR, bt % RR, T) + bt // RR + 1) * (16 * TOPK))
                nc.vector.tensor_copy(row_no[:, b, :], row_f[:]).then_inc(rows_no_ready, 1)
                restart()

            def spread(i, t):
                u = i * T + t
                b = t % RC
                dve.wait_ge(wexp_ready, u + 1)
                after(mark(nc.vector.reciprocal(wrec[:], wsum[:, b:b + 1])))
                after(mark(nc.vector.tensor_scalar(wts[:], wexp[:, b, :], wrec[:, 0:1], None, ALU.mult)))
                if not (isinstance(i, int) and i == 0 and t < 2):
                    dve.wait_ge(kv_ps, u - 1)
                nc.vector.tensor_tensor(diag[:, t % 2, :, :], ident[:].unsqueeze(1).to_broadcast([P, TOPK, P]),
                                        wts[:].unsqueeze(2).to_broadcast([P, TOPK, P]), ALU.mult).then_inc(diag_ready, 1)

            def add_part(i, t):
                u = i * T + t
                dve.wait_ge(y_ps, u + 1)
                row = xres_flat[:, t * P:(t + 1) * P]
                nc.vector.scalar_tensor_tensor(out=row, in0=ps[:, B_M, 2 * P:3 * P], scalar=rrec[:, 0:1], in1=row,
                                               op0=ALU.mult, op1=ALU.add).then_inc(y_added, 1)

            def attend(i, t, before, diag_for, ahead):
                u = i * T + t
                for c in range(chunks[t]):
                    g = chunk0[t] + c
                    w = min(512, (t + 1) * P - c * 512)
                    last = c == chunks[t] - 1
                    dve.wait_ge(s_ps, i * CPH + g + 1)
                    if not last:
                        nc.vector.tensor_scalar(prob[:, c * 512:c * 512 + w], ps[:, B_S + g % 2, 0:w], SCALE, None,
                                                ALU.mult, ALU.max, accum_out=smax[:, c:c + 1]).then_inc(s_read, 1)
                        continue
                    w -= P
                    if w:
                        mark(nc.vector.tensor_scalar(prob[:, c * 512:c * 512 + w], ps[:, B_S + g % 2, 0:w], SCALE, None,
                                                     ALU.mult, ALU.max, accum_out=smax[:, c:c + 1]))
                    k = c + (w > 0)
                    dve.sem_inc(dve_tick, 1)
                    nc.vector.tensor_tensor_reduce(
                        out=prob[:, t * P:(t + 1) * P], in0=ps[:, B_S + g % 2, w:w + P], in1=causal[:], scale=SCALE,
                        scalar=-3.4e38, op0=ALU.add, op1=ALU.max, accum_out=smax[:, k:k + 1]).then_inc(s_read, 1)
                dve.wait_ge(s_read, i * CPH + chunk0[t] + chunks[t])
                after(mark(nc.vector.tensor_reduce(rtot[:], smax[:, 0:k + 1], AX_X, ALU.max)))
                nc.vector.tensor_scalar(nmax[:], rtot[:], -1.0, None, ALU.mult).then_inc(nmax_ready, 1)
                if before is not None:
                    add_part(*before)
                if diag_for is not None:
                    spread(*diag_for)
                if ahead is not None:
                    choose(*ahead)
                if before is not None:
                    dve.wait_ge(y_added, u)
                dve.wait_ge(exp_done, i * CPH + chunk0[t] + chunks[t])
                after(mark(nc.vector.tensor_reduce(rtot[:], rpart[:, 0:chunks[t]], AX_X, ALU.add)))
                after(mark(nc.vector.reciprocal(rrec[:], rtot[:])))
                restart()

            def step(i, t, d):
                if t + d < T:
                    return (i, t + d)
                return None if isinstance(i, int) and i == NH - 1 else (i + 1, t + d - T)

            for t in range(AHEAD):
                choose(0, t)
            spread(0, 0)
            spread(0, 1)
            restart()

            def head(i):
                for t in range(T):
                    before = (i, t - 1) if t else None if isinstance(i, int) and i == 0 else (i - 1, T - 1)
                    attend(i, t, before, step(i, t, 2), step(i, t, AHEAD))

            head(0)
            with dve.Fori(1, NH - 1) as i:
                head(i)
            head(NH - 1)
            add_part(NH - 1, T - 1)


def kernel(x, adj, L0_gnn_W, L0_gnn_a, L0_gnn_gamma, L0_gnn_beta, L0_ffn_Wq_pk, L0_ffn_pk_keys, L0_ffn_Wq,
           L0_ffn_keys_table, L0_ffn_values_table, L0_ffn_Wo):
    import numpy as np
    import concourse.bacc as bacc
    from concourse.bass_utils import run_bass_kernel_spmd

    n, d = np.shape(x)
    tiles = -(-n // P)
    xp = np.zeros((tiles * P, d), np.asarray(x).dtype)
    xp[:n] = x
    xp = np.ascontiguousarray(xp.reshape(tiles, P, d).transpose(1, 0, 2))
    adjp = np.zeros((tiles * P, n), np.asarray(adj).dtype)
    adjp[:n] = adj
    a = np.asarray(L0_gnn_a)[:, 0]
    hd = a.shape[0] // 2
    gh = d // hd
    a_src = np.zeros((d, gh), a.dtype)
    a_dst = np.zeros((d, gh, P), a.dtype)
    for h in range(gh):
        a_src[h * hd:(h + 1) * hd, h] = a[:hd]
        a_dst[h * hd:(h + 1) * hd, h, :] = a[hd:, None]
    gamma = np.ascontiguousarray(np.broadcast_to(np.asarray(L0_gnn_gamma)[None, :], (P, d)))
    beta = np.ascontiguousarray(np.broadcast_to(np.asarray(L0_gnn_beta)[None, :], (P, d)))
    pk = np.asarray(L0_ffn_pk_keys)
    halves, nk, nh, dk = pk.shape
    pk_t = np.ascontiguousarray(pk.transpose(3, 2, 0, 1)).reshape(dk, nh * halves, nk)
    wqpk = np.asarray(L0_ffn_Wq_pk).reshape(d, halves, nh, dk)
    wqpk_t = np.ascontiguousarray(wqpk.transpose(3, 2, 1, 0)).reshape(dk, nh * halves, d)
    wq = np.asarray(L0_ffn_Wq).reshape(d, nh, d)
    kv = np.concatenate([np.asarray(L0_ffn_keys_table), np.asarray(L0_ffn_values_table)], axis=1)
    wo = np.ascontiguousarray(np.asarray(L0_ffn_Wo).reshape(nh, d, d).transpose(1, 0, 2))

    nc = bacc.Bacc("TRN2", target_bir_lowering=False, num_devices=1)
    arrays = {"x_rows": xp, "adj_rows": adjp, "gnn_w": np.asarray(L0_gnn_W), "a_src": a_src, "a_dst": a_dst,
              "gamma": gamma, "beta": beta, "wqpk_t": wqpk_t, "pk_t": pk_t, "wq": wq, "kv_table": kv, "wo": wo}
    args = [nc.dram_tensor(name, v.shape, mybir.dt.from_np(v.dtype), kind="ExternalInput").ap()
            for name, v in arrays.items()]
    out = nc.dram_tensor("out_rows", (tiles * P, d), F32, kind="ExternalOutput").ap()
    build(nc, *args, out)
    r = run_bass_kernel_spmd(nc, [arrays], core_ids=[0])
    return r.results[0]["out_rows"][:n]
```

```python
from contextlib import ExitStack

import concourse.bass as bass
from concourse import mybir

P = 128
ALU = mybir.AluOpType
ACT = mybir.ActivationFunctionType
AX_X = mybir.AxisListType.X
F32 = mybir.dt.float32
U32 = mybir.dt.uint32
BF16 = mybir.dt.bfloat16
RMAX = bass.bass_isa.ReduceOp.max

LN_EPS = 1e-05
ALPHA = 0.2
NEG_INF = -9000000000000000.0
CAUSAL_NEG = -3.0e38
REMOVED = -3.4e38
SPREAD = 60.0
TOPK = 16

RECTS = [(0, 1, 16), (1, 1, 8), (2, 2, 5), (4, 4, 3), (8, 8, 1)]
NCAND = sum(r * c for _, r, c in RECTS)


def build(nc, x, adj, adj_t, gnn_w, a_both, a_bcast, gamma, beta, wqpk_t, pk_t, wq, kv_table, wo, out):
    N = adj.shape[1]
    T = x.shape[1]
    NP = T * P
    GH = a_both.shape[1] // 2
    HD = P // GH
    NH = wo.shape[1]
    NUM_KV = kv_table.shape[0] // NH
    NK = pk_t.shape[2]
    DK = pk_t.shape[0]
    CH = (T + 3) // 4
    SCALE = float(P) ** -0.5
    PAIRS = T // 2
    HX = HD + 1
    SPLIT = 3 * HX
    QF = NP // 512
    RM, RG, RA = 4, 3, 3
    assert T % 2 == 0 and (T - 1) * P < N <= NP

    def width(b):
        return min(P, N - b * P)

    def chunk(c):
        return min(512, NP - c * 512)

    ACT_CHUNKS = [0, 1, 2, 3, 4, 5]
    DVE_CHUNKS = [c for c in range(CH) if c not in ACT_CHUNKS]

    RR, RC = 3, 13
    TURN = 6
    row_buf = [t % RR if t < TURN else (t - T) % RR for t in range(T)]

    def rows_fetched(i, t):
        return (i * row_buf.count(row_buf[t]) + row_buf[:t + 1].count(row_buf[t])) * (16 * TOPK)

    def row_user_before(i, t):
        users = [p for p in range(T) if row_buf[p] == row_buf[t]]
        if t > users[0]:
            return i * T + max(p for p in users if p < t)
        return None if isinstance(i, int) and i == 0 else (i - 1) * T + users[-1]

    AHEAD = 5

    def uses(r, b, t):
        return (t - b + r - 1) // r if t > b else 0

    def user_before(r, i, t, n=T):
        if t >= r:
            return i * n + t - r
        if isinstance(i, int) and i == 0:
            return None
        return (i - 1) * n + max(p for p in range(n) if p % r == t % r)

    chunks = [t // 4 + 1 for t in range(T)]
    chunk0 = [sum(chunks[:t]) for t in range(T)]
    CPH = sum(chunks)
    assert CPH % 2 == 0

    with ExitStack() as ctx:
        def sb(name, shape, dt=F32):
            return ctx.enter_context(nc.sbuf_tensor(name, shape, dt))

        def sem(name):
            return ctx.enter_context(nc.semaphore(name))

        ps = ctx.enter_context(nc.psum_tensor("ps", [P, 8, 512], F32))

        ident = sb("ident", [P, P])
        causal = sb("causal", [P, P])
        cand_no = sb("cand_no", [P, NCAND])
        head_base = sb("head_base", [P, NH])
        eps = sb("eps", [P, 1])
        w_sb = sb("w_sb", [P, P])
        a_sb = sb("a_sb", [P, 2 * GH])
        ones = sb("ones", [P, P])
        pick = sb("pick", [P, HX])
        gamma_sb = sb("gamma_sb", [P, P])
        beta_sb = sb("beta_sb", [P, P])
        wq_sb = sb("wq_sb", [P, NH, P])
        wo_sb = sb("wo_sb", [P, NH, P])
        wc_sb = sb("wc_sb", [P, 2 * NH, NK])
        wq_head = sb("wq_head", [P, P])
        xres = sb("xres", [P, T, P])
        xT = sb("xT", [P, NP])
        kT = sb("kT", [P, NP])
        v_sb = sb("v_sb", [P, T, P])
        big = sb("big", [P, 2 * NP + GH * NP + 4 * 512])
        h_sb = sb("h_sb", [P, T, P])
        z_sb = sb("z_sb", [P, 2, NP])
        sd_sb = sb("sd_sb", [P, T, 2 * GH])
        d_ext = sb("d_ext", [P, 2 * GH])
        d_all = sb("d_all", [P, 2 * GH])
        spread_h = sb("spread_h", [P, GH])
        spread_m = sb("spread_m", [P, 1])
        wide = sb("wide", [P, 1], U32)
        lonely = sb("lonely", [P, 4 * GH])
        stat = sb("stat", [P, 4, T])
        cmax = sb("cmax", [P, 2])
        lmax = sb("lmax", [P, 2])
        negc = sb("negc", [P, 2])
        rsum = sb("rsum", [P, 2])
        rinv = sb("rinv", [P, 2])
        top_val = sb("top_val", [P, 2, 2, TOPK])
        top_idx = sb("top_idx", [P, 2, TOPK], U32)
        rest = sb("rest", [P, 2, NK])
        cand = sb("cand", [P, 2, NCAND])
        cand_rest = sb("cand_rest", [P, NCAND])
        fin_val = sb("fin_val", [P, RC, TOPK])
        fin_pos = sb("fin_pos", [P, TOPK], U32)
        fin_neg = sb("fin_neg", [P, RC])
        hit = sb("hit", [P, TOPK, NCAND])
        row_f = sb("row_f", [P, TOPK])
        row_no = sb("row_no", [P, RC, TOPK], U32)
        wexp = sb("wexp", [P, RC, TOPK])
        wsum = sb("wsum", [P, RC])
        wrec = sb("wrec", [P, 1])
        wts = sb("wts", [P, TOPK])
        smax = sb("smax", [P, CH + 1])
        nmax = sb("nmax", [P, 1])
        rpart = sb("rpart", [P, CH])
        rtot = sb("rtot", [P, 1])
        rrec = sb("rrec", [P, 1])

        adj_sb = big[:, 0:2 * NP].rearrange("p (b n) -> p b n", b=2)
        d_bc = big[:, 2 * NP:(2 + GH) * NP].rearrange("p (h n) -> p h n", h=GH)
        gpt4 = big[:, (2 + GH) * NP:(2 + GH) * NP + 4 * 512].rearrange("p (b n) -> p b n", b=4)
        wqpk_sb = big[0:DK, 0:2 * NH * P].rearrange("p (h n) -> p h n", h=2 * NH)
        pk_sb = big[0:DK, NP:NP + 2 * NH * NK].rearrange("p (h n) -> p h n", h=2 * NH)
        rows_sb = big[:, 0:RR * TOPK * 256].rearrange("p (b k n) -> p b k n", b=RR, k=TOPK)
        o1 = RR * TOPK * 256
        diag = big[:, o1:o1 + 2 * TOPK * P].rearrange("p (b k n) -> p b k n", b=2, k=TOPK)
        o2 = o1 + 2 * TOPK * P
        pt_sb = big[:, o2:o2 + 1024].rearrange("p (b n) -> p b n", b=2)
        o3 = o2 + 1024
        k_tok = big[:, o3:o3 + P]
        qT = big[:, o3 + P:o3 + 2 * P]
        oT = big[:, o3 + 2 * P:o3 + 3 * P]
        prob = z_sb[:, 0, :]
        s_flat = sd_sb[:, :, :].rearrange("p t h -> p (t h)")
        a_bc = big[:, (2 + GH) * NP:(2 + GH) * NP + 2 * GH * P].rearrange("p (k h n) -> p k h n", k=2, h=GH)
        s_bc = d_bc
        hit_flat = hit[:, :, :].rearrange("p k n -> p (k n)")
        neg_d, d_off, s_off, s_off2 = (hit_flat[:, k * T * GH:(k + 1) * T * GH].rearrange("p (t h) -> p t h", t=T)
                                       for k in range(4))
        o4 = 4 * T * GH
        h_sum = hit_flat[:, o4:o4 + GH * HX].rearrange("p (h n) -> p h n", h=GH)
        v_fac = fin_val[:, :, :].rearrange("p b k -> p (b k)")[:, 0:2 * T * GH].rearrange("p (k t h) -> p k t h", k=2, t=T)
        u_fac = wexp[:, :, :].rearrange("p b k -> p (b k)")[:, 0:2 * T * GH].rearrange("p (k t h) -> p k t h", k=2, t=T)
        nsp = T * GH * SPLIT
        split_v = z_sb[:, :, :].rearrange("p b n -> p (b n)")[:, 0:nsp // 2].bitcast(BF16).rearrange(
            "p (t h k n) -> p t h k n", t=T, h=GH, k=3)
        mix = z_sb[:, :, :].rearrange("p b n -> p (b n)")[:, nsp // 2:nsp // 2 + 8 * GH * HX].rearrange(
            "p (k r n) -> p k r n", k=2, r=4 * GH)
        split_w = big[:, 0:nsp // 2].bitcast(BF16).rearrange("p (t h k n) -> p t h k n", t=T, h=GH, k=3)
        masks = big[:, (2 + GH) * NP:(2 + GH) * NP + RM * 512].bitcast(BF16).rearrange("p (b k n) -> p b k n", b=RM, k=2)
        h_flat = h_sb[:, :, :].rearrange("p t n -> p (t n)")
        gates = h_flat[:, 0:RG * GH * 256].bitcast(BF16).rearrange("p (b h n) -> p b h n", b=RG, h=GH)
        adjt_sb = xT[:, 0:RA * 1024].rearrange("p (b m n) -> p b m n", b=RA, m=2)
        sums_a = kT[:, 0:6 * 512].rearrange("p (k n) -> p k n", k=6)
        sums_b = big[:, nsp // 2:nsp // 2 + 1024].rearrange("p (k n) -> p k n", k=2)
        sv_flat = z_sb[:, :, :].rearrange("p b n -> p (b n)")[:, 0:nsp // 2].bitcast(BF16)
        sw_flat = big[:, 0:nsp // 2].bitcast(BF16)
        u_flat = u_fac[:, :, :, :].rearrange("p k t h -> p k (t h)")
        half = T // 2 * GH * HX
        scaled = xT[:, 0:half].rearrange("p (t h n) -> p t h n", t=T // 2, h=GH)
        v_flat = v_sb[:, :, :].rearrange("p t n -> p (t n)")
        xres_flat = xres[:, :, :].rearrange("p t n -> p (t n)")
        wq_flat = wq_sb[:, :, :].rearrange("p h n -> p (h n)")
        wo_flat = wo_sb[:, :, :].rearrange("p h n -> p (h n)")
        wc_pairs = wc_sb[:, :, :].rearrange("p h n -> p (h n)")
        hb_flat = head_base[:, :]
        kT3 = kT[:, :].rearrange("p (t n) -> p t n", t=T)

        x_in = sem("x_in")
        weights_in = sem("weights_in")
        eps_set = sem("eps_set")
        consts = sem("consts")
        pool_own = sem("pool_own")
        dve_own = sem("dve_own")
        act_tick = sem("act_tick")
        var_ready = sem("var_ready")
        std_ready = sem("std_ready")
        xn_ready = sem("xn_ready")
        filled = sem("filled")
        emptied = [sem("emptied_act"), sem("emptied_dve")]
        adj_in = [sem("adj_in0"), sem("adj_in1")]
        adj_used = sem("adj_used")
        ext_ready = sem("ext_ready")
        ext_all = sem("ext_all")
        offs_ready = sem("offs_ready")
        fac_ready = sem("fac_ready")
        wide_ready = sem("wide_ready")
        split_ready = sem("split_ready")
        adjt_in = [sem(f"adjt_in{b}") for b in range(RA)]
        mask_ready = sem("mask_ready")
        neg_ready = sem("neg_ready")
        gate_ready = sem("gate_ready")
        block_done = sem("block_done")
        sums_act = sem("sums_act")
        sums_dve = sem("sums_dve")
        mix_ps = sem("mix_ps")
        mix_done = sem("mix_done")
        z_ready = sem("z_ready")
        negc_ready = sem("negc_ready")
        p_ready = sem("p_ready")
        gt_ps = sem("gt_ps")
        gt_act = sem("gt_act")
        gt_dve = sem("gt_dve")
        gnn_ps = sem("gnn_ps")
        gnn_read = sem("gnn_read")
        gnn_done = sem("gnn_done")
        x3_ready = sem("x3_ready")
        x3_ps = sem("x3_ps")
        x3T_act = sem("x3T_act")
        wq_ready = sem("wq_ready")
        scores_ready = sem("scores_ready")
        scores_read = sem("scores_read")
        fin_ready = sem("fin_ready")
        wexp_ready = sem("wexp_ready")
        rows_no_ready = sem("rows_no_ready")
        rows_in = [sem(f"rows_in{b}") for b in range(RR)]
        pool_tick = sem("pool_tick")
        dve_tick = sem("dve_tick")
        diag_ready = sem("diag_ready")
        kv_ps = sem("kv_ps")
        kv_staged = sem("kv_staged")
        qk_ps = sem("qk_ps")
        qk_ready = sem("qk_ready")
        s_ps = sem("s_ps")
        s_read = sem("s_read")
        nmax_ready = sem("nmax_ready")
        exp_done = sem("exp_done")
        pt_ps = sem("pt_ps")
        pt_ready = sem("pt_ready")
        o_ps = sem("o_ps")
        o_ready = sem("o_ready")
        y_ps = sem("y_ps")
        y_added = sem("y_added")
        out_done = sem("out_done")

        block = ctx.enter_context(nc.Block())

        B_SC, B_KV, B_S, B_T, B_O, B_M = 0, 1, 2, 4, 6, 7

        F_XT, F_H, F_HT = 0, CH, 2 * CH
        F_WC = 3 * CH
        F_S = F_WC + (2 * NH + 3) // 4
        F_D = F_S + 1
        F_HS = F_D + GH * CH
        F_END = F_HS + 1
        F_DD = F_END
        F_DEND = F_DD + GH * CH

        def prologue_fill(f):
            if f < F_H:
                c = f
                return xT[:, c * 512:c * 512 + chunk(c)], chunk(c)
            if f < F_HT:
                c = f - F_H
                return h_sb[:, 4 * c:4 * c + chunk(c) // P, :].rearrange("p t n -> p (t n)"), chunk(c)
            if f < F_WC:
                c = f - F_HT
                return kT[:, c * 512:c * 512 + chunk(c)], chunk(c)
            if f < F_S:
                c = f - F_WC
                return wc_sb[:, 4 * c:4 * c + 4, :].rearrange("p h n -> p (h n)"), 4 * NK
            if f < F_D:
                return s_flat, T * 2 * GH
            if f == F_HS:
                return h_sum[:, :, 0:HD], P
            hd, c = divmod(f - (F_D if f < F_HS else F_DD), CH)
            return d_bc[:, hd, c * 512:c * 512 + chunk(c)], chunk(c)

        def need_emptied(eng, f):
            if f >= 1:
                eng.wait_ge(emptied[0], (f + 1) // 2)
            if f >= 2:
                eng.wait_ge(emptied[1], f // 2)

        @block.sync
        def _(sp):
            sp.dma_start(xres[:], x).then_inc(x_in, 16)
            for dst, src in ((w_sb[:], gnn_w), (a_sb[:], a_both), (a_bc, a_bcast), (gamma_sb[:], gamma),
                             (beta_sb[:], beta), (wqpk_sb, wqpk_t), (pk_sb, pk_t), (wq_sb[:], wq), (wo_sb[:], wo)):
                sp.dma_start(dst, src).then_inc(weights_in, 16)

            def load_factored(q, w):
                for pr in range(T // 2):
                    before = user_before(RA, q, pr, T // 2)
                    if before is not None:
                        sp.wait_ge(mask_ready, 2 * (before + 1))
                    src = adj_t[2 * pr * P:(2 * pr + 2) * P, bass.ds(q * 512, w)].rearrange("(m p) n -> p m n", p=P)
                    sp.dma_start(adjt_sb[:, pr % RA, :, 0:w], src).then_inc(adjt_in[pr % RA], 16)

            sp.wait_ge(wide_ready, 1)
            general = sp.value_load(wide[0:1, 0:1], min_val=0, max_val=1)
            with sp.If(general < 1):
                sp.wait_ge(split_ready, 1)
                load_factored(0, 512)
                with sp.Fori(1, QF) as q:
                    load_factored(q, 512)
                load_factored(QF, NP - QF * 512)
            with sp.Else():
                for b in range(2):
                    sp.dma_start(adj_sb[:, b, 0:N], adj[b * P:(b + 1) * P, :]).then_inc(adj_in[b], 16)
                with sp.Fori(1, PAIRS) as i:
                    for b in range(2):
                        sp.wait_ge(adj_used, 2 * i + b - 1)
                        sp.dma_start(adj_sb[:, b, 0:N], adj[bass.ds(i * (2 * P) + b * P, P), :]).then_inc(adj_in[b], 16)

            sp.wait_ge(y_added, T * NH)
            sp.dma_start(out.rearrange("(t p) c -> p t c", p=P), xres[:]).then_inc(out_done, 16)
            sp.wait_ge(out_done, 16)

        @block.gpsimd
        def _(pool):
            nc.gpsimd.memset(ident[:], 0.0).then_inc(pool_own, 1)
            nc.gpsimd.memset(causal[:], 0.0).then_inc(pool_own, 1)
            pool.wait_ge(pool_own, 2)
            nc.gpsimd.affine_select(out=ident[:], in_=ident[:], compare_op=ALU.not_equal, fill=1.0, base=0,
                                    pattern=[[-1, P]], channel_multiplier=1).then_inc(consts, 1)
            nc.gpsimd.affine_select(out=causal[:], in_=causal[:], compare_op=ALU.is_ge, fill=CAUSAL_NEG, base=0,
                                    pattern=[[-1, P]], channel_multiplier=1).then_inc(consts, 1)
            nc.gpsimd.iota(cand_no[:], pattern=[[1, NCAND]], base=0, channel_multiplier=0,
                           allow_small_or_imprecise_dtypes=True).then_inc(consts, 1)
            nc.gpsimd.iota(head_base[:], pattern=[[NUM_KV // 2, NH]], base=0, channel_multiplier=0,
                           allow_small_or_imprecise_dtypes=True).then_inc(consts, 1)

            nc.gpsimd.memset(ones[:], 1.0).then_inc(consts, 1)
            nc.gpsimd.memset(pick[:], 0.0).then_inc(pool_own, 1)
            for k in range(3):
                pool.wait_ge(pool_own, 3 + k)
                nc.gpsimd.affine_select(out=pick[:], in_=pick[:], compare_op=ALU.not_equal, fill=1.0, base=-HX * k,
                                        pattern=[[-1, HX]], channel_multiplier=1).then_inc(pool_own, 1)
            pool.wait_ge(ext_ready, 1)
            nc.gpsimd.partition_all_reduce(d_all[:], d_ext[:], P, RMAX).then_inc(ext_all, 1)

            def mask_blocks(q, w):
                for m in range(T):
                    pr = m // 2
                    if m % 2 == 0:
                        pool.wait_ge(adjt_in[pr % RA], (q * uses(RA, pr % RA, T // 2) + pr // RA + 1) * 16)
                        pool.sem_inc(pool_tick, 1)
                    before = user_before(RM, q, m)
                    if before is not None:
                        pool.wait_ge(block_done, before + 1)
                        pool.sem_inc(pool_tick, 1)
                    src = adjt_sb[:, pr % RA, m % 2, 0:w]
                    nc.gpsimd.tensor_scalar(masks[:, m % RM, 0, 0:w], src, 0.0, None, ALU.is_gt).then_inc(mask_ready, 1)

            pool.wait_ge(wide_ready, 1)
            general = pool.value_load(wide[0:1, 0:1], min_val=0, max_val=1)
            with pool.If(general < 1):
                mask_blocks(0, 512)
                with pool.Fori(1, QF) as q:
                    mask_blocks(q, 512)
                mask_blocks(QF, NP - QF * 512)

            def gather(i, t):
                b = row_buf[t]
                pool.wait_ge(rows_no_ready, i * T + t + 1)
                pool.sem_inc(pool_tick, 1)
                before = row_user_before(i, t)
                if before is not None:
                    pool.wait_ge(kv_ps, before + 1)
                    pool.sem_inc(pool_tick, 1)
                for k in range(TOPK):
                    nc.gpsimd.indirect_dma_start(rows_sb[:, b, k, :], None, kv_table[:, :],
                                                 bass.IndirectOffsetOnAxis(ap=row_no[:, t % RC, k:k + 1], axis=0)
                                                 ).then_inc(rows_in[b], 16)

            for t in range(T):
                gather(0, t)
            with pool.Fori(1, NH) as i:
                for t in range(T):
                    gather(i, t)

        @block.tensor
        def _(pe):
            def room(f):
                if f >= 8:
                    pe.wait_ge(emptied[f % 2], (f - 8) // 2 + 1)

            pe.wait_ge(consts, 5)
            pe.wait_ge(xn_ready, 1)
            for c in range(CH):
                f = F_XT + c
                room(f)
                for j in range(chunk(c) // P):
                    mm = pe.transpose(ps[:, f % 8, j * P:(j + 1) * P], v_sb[:, 4 * c + j, :], ident[:])
                mm.then_inc(filled, 1)
            pe.wait_ge(weights_in, 9 * 16)
            need_emptied(pe, F_H)
            for c in range(CH):
                f = F_H + c
                room(f)
                for j in range(chunk(c) // P):
                    t = 4 * c + j
                    mm = pe.matmul(ps[:, f % 8, j * P:(j + 1) * P], xT[:, t * P:(t + 1) * P], w_sb[:], start=True, stop=True)
                mm.then_inc(filled, 1)
            for c in range(CH):
                f = F_HT + c
                room(f)
                pe.matmul(ps[:, f % 8, 0:chunk(c)], w_sb[:], xT[:, c * 512:c * 512 + chunk(c)],
                          start=True, stop=True).then_inc(filled, 1)
            for c in range(2 * NH // 4):
                f = F_WC + c
                room(f)
                for j in range(4):
                    mm = pe.matmul(ps[:, f % 8, j * NK:(j + 1) * NK], wqpk_sb[:, 4 * c + j, :], pk_sb[:, 4 * c + j, :],
                                   start=True, stop=True)
                mm.then_inc(filled, 1)
            need_emptied(pe, F_WC)
            room(F_S)
            for t in range(T):
                mm = pe.matmul(ps[:, F_S % 8, t * 2 * GH:(t + 1) * 2 * GH], kT[:, t * P:(t + 1) * P], a_sb[:],
                               start=True, stop=True)
            mm.then_inc(filled, 1)

            def on_all_partitions(first, k):
                for hd in range(GH):
                    for c in range(CH):
                        f = first + hd * CH + c
                        room(f)
                        pe.matmul(ps[:, f % 8, 0:chunk(c)], a_bc[:, k, hd, :], kT[:, c * 512:c * 512 + chunk(c)],
                                  start=True, stop=True).then_inc(filled, 1)

            on_all_partitions(F_D, 0)
            room(F_HS)
            for m in range(T):
                w = width(m)
                mm = pe.matmul(ps[:, F_HS % 8, 0:P], ones[0:w, :], h_sb[0:w, m, :], start=(m == 0), stop=(m == T - 1))
            mm.then_inc(filled, 1)
            need_emptied(pe, F_END)

            def factored(q, w):
                for m in range(T):
                    pe.wait_ge(gate_ready, q * T + m + 1)
                    if m == 0 and not (isinstance(q, int) and q == 0):
                        pe.wait_ge(mix_done, q)
                    for hd in range(GH):
                        gate = gates[:, m % RG, hd, 0:w]
                        pe.matmul(ps[0:SPLIT, hd, 0:w], sv_flat[:, (m * GH + hd) * SPLIT:(m * GH + hd + 1) * SPLIT], gate,
                                  start=(m == 0), stop=(m == T - 1))
                        pe.matmul(ps[0:SPLIT, GH + hd, 0:w], sw_flat[:, (m * GH + hd) * SPLIT:(m * GH + hd + 1) * SPLIT], gate,
                                  start=(m == 0), stop=False)
                        mm = pe.matmul(ps[0:SPLIT, GH + hd, 0:w], sw_flat[:, (m * GH + hd) * SPLIT:(m * GH + hd + 1) * SPLIT],
                                       masks[:, m % RM, 0, 0:w], start=False, stop=(m == T - 1))
                    mm.then_inc(block_done, 1)
                pe.wait_ge(sums_act, (q + 1) * GH)
                pe.wait_ge(sums_dve, (q + 1) * GH)
                for j in range(w // P):
                    for k in range(2 * GH):
                        src = sums_a[0:SPLIT, k, :] if k < 6 else sums_b[0:SPLIT, k - 6, :]
                        mm = pe.matmul(ps[:, j, k * HX:(k + 1) * HX], src[:, j * P:(j + 1) * P], pick[0:SPLIT, :],
                                       start=True, stop=True)
                    mm.then_inc(mix_ps, 1)

            def gnn_unit(it, u):
                n = it * 8 + u
                hd = u % GH
                b = u % 2

                def turn(c):
                    for j in range(chunk(c) // P):
                        m = 4 * c + j
                        w = width(m)
                        mm = pe.transpose(ps[0:w, c % 4, j * P:(j + 1) * P], z_sb[:, b, m * P:m * P + w], ident[:])
                    mm.then_inc(gt_ps, 1)

                def times_h(c):
                    if c in ACT_CHUNKS:
                        pe.wait_ge(gt_act, n * len(ACT_CHUNKS) + ACT_CHUNKS.index(c) + 1)
                    else:
                        pe.wait_ge(gt_dve, n * len(DVE_CHUNKS) + DVE_CHUNKS.index(c) + 1)
                    for j in range(chunk(c) // P):
                        m = 4 * c + j
                        w = width(m)
                        mm = pe.matmul(ps[:, 6 + b, 0:HD], gpt4[0:w, c % 4, j * P:(j + 1) * P],
                                       h_sb[0:w, m, hd * HD:(hd + 1) * HD], start=(m == 0), stop=(m == T - 1))
                    return mm

                pe.wait_ge(p_ready, n + 1)
                turn(0)
                turn(1)
                for c in range(CH):
                    if c == 0 and not (isinstance(it, int) and u < 2):
                        pe.wait_ge(gnn_read, n - 1)
                    mm = times_h(c)
                    if c + 2 < CH:
                        turn(c + 2)
                mm.then_inc(gnn_ps, 1)

            pe.wait_ge(wide_ready, 1)
            general = pe.value_load(wide[0:1, 0:1], min_val=0, max_val=1)
            with pe.If(general < 1):
                factored(0, 512)
                with pe.Fori(1, QF) as q:
                    factored(q, 512)
                factored(QF, NP - QF * 512)
            with pe.Else():
                on_all_partitions(F_DD, 1)
                need_emptied(pe, F_DEND)
                for u in range(8):
                    gnn_unit(0, u)
                with pe.Fori(1, PAIRS) as it:
                    for u in range(8):
                        gnn_unit(it, u)

            pe.wait_ge(x3_ready, 1)
            for c in range(CH):
                if c >= 2:
                    pe.wait_ge(x3T_act, c - 1)
                for j in range(chunk(c) // P):
                    mm = pe.transpose(ps[:, c % 2, j * P:(j + 1) * P], z_sb[:, 0, (4 * c + j) * P:(4 * c + j + 1) * P], ident[:])
                mm.then_inc(x3_ps, 1)
            pe.wait_ge(x3T_act, CH)

            def scores(i, t):
                if not (t == 0 and isinstance(i, int) and i == 0):
                    pe.wait_ge(scores_read, i * T + t)
                pe.matmul(ps[:, B_SC, 0:2 * NK], xT[:, t * P:(t + 1) * P],
                          wc_pairs[:, bass.ds(i * 2 * NK, 2 * NK)], start=True, stop=True).then_inc(scores_ready, 1)

            def sum_rows(i, t):
                u = i * T + t
                pe.wait_ge(diag_ready, u + 1)
                pe.wait_ge(rows_in[row_buf[t]], rows_fetched(i, t))
                if not (isinstance(i, int) and i == 0 and t == 0):
                    pe.wait_ge(kv_staged, 2 * u)
                for k in range(TOPK):
                    mm = pe.matmul(ps[:, B_KV, 0:256], diag[:, t % 2, k, :], rows_sb[:, row_buf[t], k, :],
                                   start=(k == 0), stop=(k == TOPK - 1))
                mm.then_inc(kv_ps, 1)

            def queries_keys(i, t):
                u = i * T + t
                if t == 0:
                    pe.wait_ge(wq_ready, i + 1)
                if not (isinstance(i, int) and i == 0 and t < 2):
                    pe.wait_ge(y_added, u - 1)
                elif t == 1:
                    pe.wait_ge(qk_ready, 2)
                pe.matmul(ps[:, B_M, 0:P], wq_head[:], xT[:, t * P:(t + 1) * P], start=True, stop=True)
                pe.wait_ge(kv_staged, 2 * u + 1)
                pe.transpose(ps[:, B_M, P:2 * P], k_tok, ident[:]).then_inc(qk_ps, 1)

            def out_part(i, t):
                pe.wait_ge(o_ready, i * T + t + 1)
                pe.matmul(ps[:, B_M, 2 * P:3 * P], oT, wo_flat[:, bass.ds(i * P, P)], start=True, stop=True).then_inc(y_ps, 1)

            def attend(i, t, before, nxt, ahead):
                u = i * T + t
                pe.wait_ge(qk_ready, 2 * u + 2)
                for c in range(chunks[t]):
                    g = chunk0[t] + c
                    if not (g < 2 and isinstance(i, int) and i == 0):
                        pe.wait_ge(s_read, i * CPH + g - 1)
                    w = min(512, (t + 1) * P - c * 512)
                    pe.matmul(ps[:, B_S + g % 2, 0:w], qT, kT[:, c * 512:c * 512 + w], start=True, stop=True).then_inc(s_ps, 1)
                    if c == 0 and before is not None:
                        out_part(*before)
                if ahead is not None:
                    scores(*ahead)
                if nxt is not None:
                    sum_rows(*nxt)
                    queries_keys(*nxt)

                def turn(c):
                    pe.wait_ge(exp_done, i * CPH + chunk0[t] + c + 1)
                    w = min(4, t + 1 - 4 * c)
                    for j in range(w):
                        mm = pe.transpose(ps[:, B_T + (chunk0[t] + c) % 2, j * P:(j + 1) * P],
                                          prob[:, (4 * c + j) * P:(4 * c + j + 1) * P], ident[:])
                    mm.then_inc(pt_ps, 1)

                turn(0)
                pe.wait_ge(kv_staged, 2 * u + 2)
                for c in range(chunks[t]):
                    if c + 1 < chunks[t]:
                        turn(c + 1)
                    pe.wait_ge(pt_ready, i * CPH + chunk0[t] + c + 1)
                    for j in range(min(4, t + 1 - 4 * c)):
                        m = 4 * c + j
                        mm = pe.matmul(ps[:, B_O, 0:P], v_sb[:, m, :], pt_sb[:, (chunk0[t] + c) % 2, j * P:(j + 1) * P],
                                       start=(m == 0), stop=(m == t))
                mm.then_inc(o_ps, 1)

            def step(i, t, d):
                if t + d < T:
                    return (i, t + d)
                return None if isinstance(i, int) and i == NH - 1 else (i + 1, t + d - T)

            for t in range(AHEAD):
                scores(0, t)
            sum_rows(0, 0)
            queries_keys(0, 0)

            def head(i):
                for t in range(T):
                    before = (i, t - 1) if t else None if isinstance(i, int) and i == 0 else (i - 1, T - 1)
                    attend(i, t, before, step(i, t, 1), step(i, t, AHEAD))

            head(0)
            with pe.Fori(1, NH - 1) as i:
                head(i)
            head(NH - 1)
            pe.wait_ge(y_added, T * NH - 1)
            out_part(NH - 1, T - 1)

        @block.scalar
        def _(act):
            act.wait_ge(var_ready, 1)
            nc.scalar.activation(stat[:, 2, :], stat[:, 1, :], ACT.Sqrt, bias=eps[:], scale=1.0 / P).then_inc(std_ready, 1)
            for f in range(0, F_END, 2):
                dst, w = prologue_fill(f)
                act.wait_ge(filled, f + 1)
                nc.scalar.copy(dst, ps[:, f % 8, 0:w]).then_inc(emptied[0], 1)

            def softmax(it, u):
                n = it * 8 + u
                b = u % 2
                act.wait_ge(z_ready, n + 1)
                act.wait_ge(negc_ready, n + 1)
                nc.scalar.activation(z_sb[:, b, 0:N], z_sb[:, b, 0:N], ACT.Exp, bias=negc[:, b:b + 1],
                                     accum_out=rsum[:, b:b + 1]).then_inc(p_ready, 1)

            def copies(it, u):
                n = it * 8 + u
                for j, c in enumerate(ACT_CHUNKS):
                    act.wait_ge(gt_ps, n * CH + c + 1)
                    nc.scalar.copy(gpt4[:, c % 4, 0:chunk(c)], ps[:, c % 4, 0:chunk(c)]).then_inc(gt_act, 1)

            act.wait_ge(offs_ready, 1)
            nc.scalar.activation(v_fac[:, 0, :, :], d_off[:], ACT.Exp).then_inc(fac_ready, 1)
            nc.scalar.activation(v_fac[:, 1, :, :], d_off[:], ACT.Exp, scale=ALPHA).then_inc(fac_ready, 1)
            act.wait_ge(offs_ready, 2)
            nc.scalar.activation(u_fac[:], u_fac[:], ACT.Exp).then_inc(fac_ready, 1)

            def stage_sums(q, w):
                for m in range(T):
                    act.wait_ge(mask_ready, q * T + m + 1)
                    nc.scalar.mul(masks[:, m % RM, 1, 0:w], masks[:, m % RM, 0, 0:w], -1.0).then_inc(neg_ready, 1)
                act.wait_ge(block_done, (q + 1) * T)
                for k in range(GH):
                    nc.scalar.copy(sums_a[0:SPLIT, k, 0:w], ps[0:SPLIT, k, 0:w]).then_inc(sums_act, 1)

            act.wait_ge(wide_ready, 1)
            general = act.value_load(wide[0:1, 0:1], min_val=0, max_val=1)
            with act.If(general < 1):
                stage_sums(0, 512)
                with act.Fori(1, QF) as q:
                    stage_sums(q, 512)
                stage_sums(QF, NP - QF * 512)
            with act.Else():
                for f in range(F_DD + F_DD % 2, F_DEND, 2):
                    dst, w = prologue_fill(f)
                    act.wait_ge(filled, f + 1)
                    nc.scalar.copy(dst, ps[:, f % 8, 0:w]).then_inc(emptied[0], 1)
                need_emptied(act, F_DEND)
                for u in range(8):
                    softmax(0, u)
                    copies(0, u)
                with act.Fori(1, PAIRS) as it:
                    for u in range(8):
                        softmax(it, u)
                        copies(it, u)

            for k in range(2):
                act.wait_ge(var_ready, 2 + k)
                nc.scalar.activation(stat[:, 2, :], stat[:, 1, :], ACT.Sqrt, bias=eps[:], scale=1.0 / P).then_inc(std_ready, 1)
            for c in range(CH):
                act.wait_ge(x3_ps, c + 1)
                nc.scalar.copy(xT[:, c * 512:c * 512 + chunk(c)], ps[:, c % 2, 0:chunk(c)]).then_inc(x3T_act, 1)

            def weights(i, t):
                b = t % RC
                act.wait_ge(fin_ready, i * T + t + 1)
                nc.scalar.activation(wexp[:, b, :], fin_val[:, b, :], ACT.Exp, bias=fin_neg[:, b:b + 1],
                                     accum_out=wsum[:, b:b + 1]).then_inc(wexp_ready, 1)

            def values(i, t):
                nc.scalar.copy(v_sb[:, t, :], ps[:, B_KV, P:2 * P]).then_inc(kv_staged, 1)

            def keys_values(i, t):
                u = i * T + t
                if t == 0:
                    if not (isinstance(i, int) and i == 0):
                        act.wait_ge(qk_ps, u)
                        act.sem_inc(act_tick, 1)
                    nc.scalar.copy(wq_head[:], wq_flat[:, bass.ds(i * P, P)]).then_inc(wq_ready, 1)
                act.wait_ge(kv_ps, u + 1)
                nc.scalar.copy(k_tok, ps[:, B_KV, 0:P]).then_inc(kv_staged, 1)
                if t > 0 or (isinstance(i, int) and i == 0):
                    values(i, t)
                act.wait_ge(qk_ps, u + 1)
                nc.scalar.copy(qT, ps[:, B_M, 0:P]).then_inc(qk_ready, 1)
                nc.scalar.copy(kT[:, t * P:(t + 1) * P], ps[:, B_M, P:2 * P]).then_inc(qk_ready, 1)

            def attend(i, t, nxt, ahead):
                u = i * T + t
                act.wait_ge(nmax_ready, u + 1)
                for c in range(chunks[t]):
                    w = min(512, (t + 1) * P - c * 512)
                    nc.scalar.activation(prob[:, c * 512:c * 512 + w], prob[:, c * 512:c * 512 + w], ACT.Exp,
                                         bias=nmax[:], accum_out=rpart[:, c:c + 1]).then_inc(exp_done, 1)
                if nxt is not None:
                    keys_values(*nxt)
                for c in range(chunks[t]):
                    g = chunk0[t] + c
                    w = min(512, (t + 1) * P - c * 512)
                    act.wait_ge(pt_ps, i * CPH + g + 1)
                    nc.scalar.copy(pt_sb[:, g % 2, 0:w], ps[:, B_T + g % 2, 0:w]).then_inc(pt_ready, 1)
                act.wait_ge(o_ps, u + 1)
                nc.scalar.copy(oT, ps[:, B_O, 0:P]).then_inc(o_ready, 1)
                if t == T - 1 and nxt is not None:
                    values(*nxt)
                if ahead is not None:
                    weights(*ahead)

            def step(i, t, d):
                if t + d < T:
                    return (i, t + d)
                return None if isinstance(i, int) and i == NH - 1 else (i + 1, t + d - T)

            for t in range(AHEAD):
                weights(0, t)
            keys_values(0, 0)

            def head(i):
                for t in range(T):
                    attend(i, t, step(i, t, 1), step(i, t, AHEAD))

            head(0)
            with act.Fori(1, NH - 1) as i:
                head(i)
            head(NH - 1)

        @block.vector
        def _(dve):
            own = [0]

            def mark(ins):
                own[0] += 1
                ins.then_inc(dve_own, 1)
                return own[0]

            def after(n):
                dve.wait_ge(dve_own, n)

            def restart():
                after(own[0])
                dve.sem_clear(dve_own)
                own[0] = 0

            def bc(ap):
                return ap.unsqueeze(2).to_broadcast([P, T, P])

            def norm(dst, src, k):
                after(mark(nc.vector.tensor_reduce(stat[:, 0, :], src, AX_X, ALU.add)))
                after(mark(nc.vector.tensor_scalar(stat[:, 0, :], stat[:, 0, :], 1.0 / P, None, ALU.mult)))
                after(mark(nc.vector.tensor_tensor(dst, src, bc(stat[:, 0, :]), ALU.subtract)))
                after(mark(nc.vector.tensor_tensor(kT3, dst, dst, ALU.mult)))
                nc.vector.tensor_reduce(stat[:, 1, :], kT3, AX_X, ALU.add).then_inc(var_ready, 1)
                dve.wait_ge(std_ready, k)
                after(mark(nc.vector.reciprocal(stat[:, 3, :], stat[:, 2, :])))
                return nc.vector.tensor_tensor(dst, dst, bc(stat[:, 3, :]), ALU.mult)

            after(mark(nc.vector.memset(eps[:], LN_EPS)))
            dve.wait_ge(x_in, 16)
            norm(v_sb[:], xres[:], 1).then_inc(xn_ready, 1)
            for f in range(1, F_END, 2):
                dst, w = prologue_fill(f)
                dve.wait_ge(filled, f + 1)
                nc.vector.tensor_copy(dst, ps[:, f % 8, 0:w]).then_inc(emptied[1], 1)
            dve.wait_ge(consts, 5)
            after(mark(nc.vector.tensor_scalar(head_base[:], head_base[:], 2.0, None, ALU.mult)))
            need_emptied(dve, F_END)
            dt = sd_sb[:, :, GH:2 * GH].rearrange("p t h -> p h t")
            after(mark(nc.vector.tensor_reduce(d_ext[:, 0:GH], dt, AX_X, ALU.max)))
            after(mark(nc.vector.tensor_scalar(neg_d[:], sd_sb[:, :, GH:2 * GH], -1.0, None, ALU.mult)))
            nc.vector.tensor_reduce(d_ext[:, GH:2 * GH], neg_d[:].rearrange("p t h -> p h t"), AX_X, ALU.max).then_inc(ext_ready, 1)
            dve.wait_ge(ext_all, 1)
            after(mark(nc.vector.tensor_tensor(spread_h[:], d_all[:, 0:GH], d_all[:, GH:2 * GH], ALU.add)))
            after(mark(nc.vector.tensor_reduce(spread_m[:], spread_h[:], AX_X, ALU.max)))
            nc.vector.tensor_scalar(wide[:], spread_m[:], SPREAD, None, ALU.is_gt).then_inc(wide_ready, 1)
            top = d_all[:, 0:GH].unsqueeze(1).to_broadcast([P, T, GH])
            nc.vector.tensor_tensor(d_off[:], sd_sb[:, :, GH:2 * GH], top, ALU.subtract).then_inc(offs_ready, 1)
            after(mark(nc.vector.tensor_tensor(s_off[:], sd_sb[:, :, 0:GH], top, ALU.add)))
            lk = mark(nc.vector.scalar_tensor_tensor(out=s_off2[:], in0=s_off[:], scalar=ALPHA, in1=s_off[:],
                                                     op0=ALU.mult, op1=ALU.max))
            after(lk)
            after(mark(nc.vector.tensor_tensor(u_fac[:, 0, :, :], s_off[:], s_off2[:], ALU.subtract)))
            nc.vector.scalar_tensor_tensor(out=u_fac[:, 1, :, :], in0=s_off[:], scalar=ALPHA, in1=s_off2[:],
                                           op0=ALU.mult, op1=ALU.subtract).then_inc(offs_ready, 1)
            after(mark(nc.vector.memset(h_sum[:, :, HD:HX], float(N))))
            restart()

            def mask_row(it, u):
                tt = u // GH
                dve.wait_ge(adj_in[tt], it * 16 + 16)
                return mark(nc.vector.tensor_scalar(adj_sb[:, tt, 0:N], adj_sb[:, tt, 0:N], 0.0, NEG_INF,
                                                    ALU.is_le, ALU.mult))

            def logits(it, u):
                n = it * 8 + u
                hd, b, tt = u % GH, u % 2, u // GH
                if hd == 0:
                    m = mask_row(it, u)
                else:
                    m = 0
                if not (isinstance(it, int) and u < 2):
                    dve.wait_ge(gnn_ps, n - 1)
                dve.sem_inc(dve_tick, 1)
                if m:
                    after(m)
                z = z_sb[:, b, 0:N]
                s_col = s_flat[:, bass.ds(it * (4 * GH) + (u // GH) * 2 * GH + hd, 1)]
                after(mark(nc.vector.tensor_scalar(z, adj_sb[:, tt, 0:N], s_col, None, ALU.add)))
                after(mark(nc.vector.tensor_tensor_reduce(out=z, in0=d_bc[:, hd, 0:N], in1=z, scale=1.0, scalar=-3.4e38,
                                                          op0=ALU.add, op1=ALU.max, accum_out=cmax[:, b:b + 1])))
                nc.vector.scalar_tensor_tensor(out=z, in0=z, scalar=ALPHA, in1=z, op0=ALU.mult,
                                               op1=ALU.max).then_inc(z_ready, 1)
                after(mark(nc.vector.scalar_tensor_tensor(out=lmax[:, b:b + 1], in0=cmax[:, b:b + 1], scalar=ALPHA,
                                                          in1=cmax[:, b:b + 1], op0=ALU.mult, op1=ALU.max)))
                nc.vector.tensor_scalar(negc[:, b:b + 1], lmax[:, b:b + 1], -1.0, None, ALU.mult).then_inc(negc_ready, 1)
                if hd == GH - 1:
                    dve.sem_inc(adj_used, 1)

            def collect(it, u):
                n = it * 8 + u
                hd, b, tt = u % GH, u % 2, u // GH
                for c in DVE_CHUNKS:
                    dve.wait_ge(gt_ps, n * CH + c + 1)
                    nc.vector.tensor_copy(gpt4[:, c % 4, 0:chunk(c)], ps[:, c % 4, 0:chunk(c)]).then_inc(gt_dve, 1)
                dve.wait_ge(p_ready, n + 1)
                after(mark(nc.vector.reciprocal(rinv[:, b:b + 1], rsum[:, b:b + 1])))
                dve.wait_ge(gnn_ps, n + 1)
                nc.vector.tensor_scalar(v_flat[:, bass.ds(n * HD, HD)], ps[:, 6 + b, 0:HD], rinv[:, b:b + 1], None,
                                        ALU.mult).then_inc(gnn_read, 1)

            def split(k, dst):
                n = T // 2
                for t0 in (0, n):
                    fac = v_fac[:, k, t0:t0 + n, :]
                    out_h = scaled[:, :, :, 0:HD]
                    mark(nc.vector.tensor_tensor(out_h, h_sb[:, t0:t0 + n, :].rearrange("p t (h n) -> p t h n", h=GH),
                                                 fac.unsqueeze(3).to_broadcast([P, n, GH, HD]), ALU.mult))
                    after(mark(nc.vector.tensor_copy(scaled[:, :, :, HD:HX].rearrange("p t h o -> p t (h o)"), fac)))
                    for part in range(3):
                        to = dst[:, t0:t0 + n, :, part, :]
                        after(mark(nc.vector.tensor_copy(to, scaled)))
                        if part < 2:
                            after(mark(nc.vector.tensor_tensor(scaled, scaled, to, ALU.subtract)))

            def gate_block(q, w, m):
                dve.wait_ge(neg_ready, q * T + m + 1)
                before = user_before(RG, q, m)
                if before is not None:
                    dve.wait_ge(block_done, before + 1)
                for hd in range(GH):
                    ins = nc.vector.scalar_tensor_tensor(
                        out=gates[:, m % RG, hd, 0:w], in0=s_bc[:, hd, bass.ds(q * 512, w)],
                        scalar=neg_d[:, m, hd:hd + 1], in1=masks[:, m % RM, 1, 0:w], op0=ALU.is_gt, op1=ALU.mult)
                ins.then_inc(gate_ready, 1)

            def gate_blocks(q, w, first, last):
                for m in range(first, last):
                    gate_block(q, w, m)

            def mix_rows(q, w, w_next):
                dve.wait_ge(block_done, (q + 1) * T)
                for k in range(GH, 2 * GH):
                    dst = sums_a[0:SPLIT, k, 0:w] if k < 6 else sums_b[0:SPLIT, k - 6, 0:w]
                    nc.vector.tensor_copy(dst, ps[0:SPLIT, k, 0:w]).then_inc(sums_dve, 1)
                if w_next:
                    gate_blocks(q + 1, w_next, 0, RG)
                nj = w // P
                nr = nj * GH
                dve.wait_ge(mix_ps, q * 4 + nj)
                for k in range(2):
                    u_row = u_flat[:, k, bass.ds(q * (4 * GH), nr)].rearrange("p (j h) -> p j h", j=nj).unsqueeze(3)
                    part = ps[:, 0:nj, k * GH * HX:(k + 1) * GH * HX].rearrange("p j (h n) -> p j h n", h=GH)
                    to = mix[:, k, 0:nr, :].rearrange("p (j h) n -> p j h n", j=nj)
                    last = mark(nc.vector.tensor_tensor(to, part, u_row.to_broadcast([P, nj, GH, HX]), ALU.mult))
                after(last)
                dve.sem_inc(mix_done, 1)
                m0, m1 = mix[:, 0, 0:nr, :], mix[:, 1, 0:nr, :]
                after(mark(nc.vector.tensor_tensor(m0, m1, m0, ALU.subtract)))
                den = mix[:, 0, 0:nr, HD:HX].rearrange("p r o -> p (r o)")
                after(mark(nc.vector.tensor_scalar(lonely[:, 0:nr], den, 0.0, None, ALU.is_equal)))
                after(mark(nc.vector.tensor_tensor(
                    m1.rearrange("p (j h) n -> p j h n", j=nj), h_sum[:].unsqueeze(1).to_broadcast([P, nj, GH, HX]),
                    lonely[:, 0:nr].rearrange("p (j h) -> p j h", j=nj).unsqueeze(3).to_broadcast([P, nj, GH, HX]), ALU.mult)))
                after(mark(nc.vector.tensor_tensor(m0, m0, m1, ALU.add)))
                after(mark(nc.vector.reciprocal(lonely[:, 0:nr], den)))
                o = v_flat[:, bass.ds(q * (4 * P), nj * P)].rearrange("p (r n) -> p r n", r=nr)
                after(mark(nc.vector.tensor_tensor(o, mix[:, 0, 0:nr, 0:HD], lonely[:, 0:nr].unsqueeze(2).to_broadcast([P, nr, HD]),
                                                   ALU.mult)))
                restart()

            general = dve.value_load(wide[0:1, 0:1], min_val=0, max_val=1)
            with dve.If(general < 1):
                dve.wait_ge(fac_ready, 3)
                split(0, split_v)
                split(1, split_w)
                dve.sem_inc(split_ready, 1)
                restart()
                w_last = NP - QF * 512
                gate_blocks(0, 512, 0, T)
                mix_rows(0, 512, 512)
                with dve.Fori(1, QF - 1) as q:
                    gate_blocks(q, 512, RG, T)
                    mix_rows(q, 512, 512)
                gate_blocks(QF - 1, 512, RG, T)
                mix_rows(QF - 1, 512, w_last)
                gate_blocks(QF, w_last, RG, T)
                mix_rows(QF, w_last, 0)
            with dve.Else():
                for f in range(F_DD + (F_DD + 1) % 2, F_DEND, 2):
                    dst, w = prologue_fill(f)
                    dve.wait_ge(filled, f + 1)
                    nc.vector.tensor_copy(dst, ps[:, f % 8, 0:w]).then_inc(emptied[1], 1)
                need_emptied(dve, F_DEND)
                logits(0, 0)
                for u in range(1, 8):
                    logits(0, u)
                    collect(0, u - 1)
                restart()
                with dve.Fori(1, PAIRS) as it:
                    for u in range(8):
                        logits(it, u)
                        if u == 0:
                            collect(it - 1, 7)
                        else:
                            collect(it, u - 1)
                    dve.sem_inc(dve_tick, 1)
                    restart()
                collect(PAIRS - 1, 7)
                dve.wait_ge(gnn_read, 4 * T)
                dve.sem_inc(dve_tick, 1)
                restart()

            dve.wait_ge(weights_in, 9 * 16)
            after(mark(norm(v_sb[:], v_sb[:], 2)))
            g_bc = gamma_sb[:].unsqueeze(1).to_broadcast([P, T, P])
            b_bc = beta_sb[:].unsqueeze(1).to_broadcast([P, T, P])
            after(mark(nc.vector.tensor_tensor(v_sb[:], v_sb[:], g_bc, ALU.mult)))
            after(mark(nc.vector.tensor_tensor(v_sb[:], v_sb[:], b_bc, ALU.add)))
            after(mark(nc.vector.tensor_tensor(xres[:], xres[:], v_sb[:], ALU.add)))
            norm(z_sb[:, 0, :].rearrange("p (t n) -> p t n", t=T), xres[:], 3).then_inc(x3_ready, 1)
            restart()

            def top16(dst, idx, src, spare, first_done=None):
                a = mark(nc.vector.max(dst[:, 0:8], src))
                after(a)
                b = mark(nc.vector.max_index(idx[:, 0:8], dst[:, 0:8], src))
                c = mark(nc.vector.match_replace(spare, dst[:, 0:8], src, REMOVED))
                after(c)
                d = mark(nc.vector.max(dst[:, 8:16], spare))
                after(d)
                return mark(nc.vector.max_index(idx[:, 8:16], dst[:, 8:16], spare))

            def choose(i, t):
                u = i * T + t
                dve.wait_ge(scores_ready, u + 1)
                dve.sem_inc(dve_tick, 1)
                for half in range(2):
                    top16(top_val[:, half, 0, :], top_idx[:, half, :], ps[:, B_SC, half * NK:(half + 1) * NK], rest[:, half, :])
                after(own[0])
                dve.sem_inc(scores_read, 1)
                a = mark(nc.vector.tensor_scalar(top_val[:, 0, 1, :], top_idx[:, 0, :], hb_flat[:, bass.ds(i, 1)], None, ALU.add))
                b = mark(nc.vector.tensor_scalar(top_val[:, 1, 1, :], top_idx[:, 1, :], float(NK), None, ALU.mult))
                after(b)
                at = 0
                for i0, r, c in RECTS:
                    a0 = top_val[:, 0, :, i0:i0 + r].unsqueeze(3).to_broadcast([P, 2, r, c])
                    a1 = top_val[:, 1, :, 0:c].unsqueeze(2).to_broadcast([P, 2, r, c])
                    o = cand[:, :, at:at + r * c].rearrange("p k (r c) -> p k r c", r=r)
                    if r == 1:
                        a0 = top_val[:, 0, :, i0:i0 + 1].to_broadcast([P, 2, c])
                        a1 = top_val[:, 1, :, 0:c]
                        o = cand[:, :, at:at + c]
                    elif c == 1:
                        a0 = top_val[:, 0, :, i0:i0 + r]
                        a1 = top_val[:, 1, :, 0:1].to_broadcast([P, 2, r])
                        o = cand[:, :, at:at + r]
                    d = mark(nc.vector.tensor_tensor(o, a0, a1, ALU.add))
                    at += r * c
                after(d)
                b = t % RC
                before = user_before(RC, i, t)
                if before is not None:
                    dve.wait_ge(wexp_ready, before + 1)
                    dve.sem_inc(dve_tick, 1)
                top16(fin_val[:, b, :], fin_pos, cand[:, 0, :], cand_rest[:])
                after(own[0])
                nc.vector.tensor_scalar(fin_neg[:, b:b + 1], fin_val[:, b, 0:1], -1.0, None, ALU.mult).then_inc(fin_ready, 1)
                after(mark(nc.vector.tensor_tensor(hit[:], fin_pos[:].unsqueeze(2).to_broadcast([P, TOPK, NCAND]),
                                                   cand_no[:].unsqueeze(1).to_broadcast([P, TOPK, NCAND]), ALU.is_equal)))
                after(mark(nc.vector.tensor_tensor(hit[:], hit[:], cand[:, 1, :].unsqueeze(1).to_broadcast([P, TOPK, NCAND]),
                                                   ALU.mult)))
                after(mark(nc.vector.tensor_reduce(row_f[:], hit[:], AX_X, ALU.add)))
                if before is not None:
                    bt = t - RC if t >= RC else max(p for p in range(T) if p % RC == t % RC)
                    bi = i if t >= RC else i - 1
                    dve.wait_ge(rows_in[row_buf[bt]], rows_fetched(bi, bt))
                nc.vector.tensor_copy(row_no[:, b, :], row_f[:]).then_inc(rows_no_ready, 1)
                restart()

            def spread(i, t):
                u = i * T + t
                b = t % RC
                dve.wait_ge(wexp_ready, u + 1)
                after(mark(nc.vector.reciprocal(wrec[:], wsum[:, b:b + 1])))
                after(mark(nc.vector.tensor_scalar(wts[:], wexp[:, b, :], wrec[:, 0:1], None, ALU.mult)))
                if not (isinstance(i, int) and i == 0 and t < 2):
                    dve.wait_ge(kv_ps, u - 1)
                nc.vector.tensor_tensor(diag[:, t % 2, :, :], ident[:].unsqueeze(1).to_broadcast([P, TOPK, P]),
                                        wts[:].unsqueeze(2).to_broadcast([P, TOPK, P]), ALU.mult).then_inc(diag_ready, 1)

            def add_part(i, t):
                u = i * T + t
                dve.wait_ge(y_ps, u + 1)
                row = xres_flat[:, t * P:(t + 1) * P]
                nc.vector.scalar_tensor_tensor(out=row, in0=ps[:, B_M, 2 * P:3 * P], scalar=rrec[:, 0:1], in1=row,
                                               op0=ALU.mult, op1=ALU.add).then_inc(y_added, 1)

            def attend(i, t, before, diag_for, ahead):
                u = i * T + t
                for c in range(chunks[t]):
                    g = chunk0[t] + c
                    w = min(512, (t + 1) * P - c * 512)
                    last = c == chunks[t] - 1
                    dve.wait_ge(s_ps, i * CPH + g + 1)
                    if not last:
                        nc.vector.tensor_scalar(prob[:, c * 512:c * 512 + w], ps[:, B_S + g % 2, 0:w], SCALE, None,
                                                ALU.mult, ALU.max, accum_out=smax[:, c:c + 1]).then_inc(s_read, 1)
                        continue
                    w -= P
                    if w:
                        mark(nc.vector.tensor_scalar(prob[:, c * 512:c * 512 + w], ps[:, B_S + g % 2, 0:w], SCALE, None,
                                                     ALU.mult, ALU.max, accum_out=smax[:, c:c + 1]))
                    k = c + (w > 0)
                    dve.sem_inc(dve_tick, 1)
                    nc.vector.tensor_tensor_reduce(
                        out=prob[:, t * P:(t + 1) * P], in0=ps[:, B_S + g % 2, w:w + P], in1=causal[:], scale=SCALE,
                        scalar=-3.4e38, op0=ALU.add, op1=ALU.max, accum_out=smax[:, k:k + 1]).then_inc(s_read, 1)
                dve.wait_ge(s_read, i * CPH + chunk0[t] + chunks[t])
                after(mark(nc.vector.tensor_reduce(rtot[:], smax[:, 0:k + 1], AX_X, ALU.max)))
                nc.vector.tensor_scalar(nmax[:], rtot[:], -1.0, None, ALU.mult).then_inc(nmax_ready, 1)
                if before is not None:
                    add_part(*before)
                if diag_for is not None:
                    spread(*diag_for)
                if ahead is not None:
                    choose(*ahead)
                if before is not None:
                    dve.wait_ge(y_added, u)
                dve.wait_ge(exp_done, i * CPH + chunk0[t] + chunks[t])
                after(mark(nc.vector.tensor_reduce(rtot[:], rpart[:, 0:chunks[t]], AX_X, ALU.add)))
                after(mark(nc.vector.reciprocal(rrec[:], rtot[:])))
                restart()

            def step(i, t, d):
                if t + d < T:
                    return (i, t + d)
                return None if isinstance(i, int) and i == NH - 1 else (i + 1, t + d - T)

            for t in range(AHEAD):
                choose(0, t)
            spread(0, 0)
            spread(0, 1)
            restart()

            def head(i):
                for t in range(T):
                    before = (i, t - 1) if t else None if isinstance(i, int) and i == 0 else (i - 1, T - 1)
                    attend(i, t, before, step(i, t, 2), step(i, t, AHEAD))

            head(0)
            with dve.Fori(1, NH - 1) as i:
                head(i)
            head(NH - 1)
            add_part(NH - 1, T - 1)


def kernel(x, adj, L0_gnn_W, L0_gnn_a, L0_gnn_gamma, L0_gnn_beta, L0_ffn_Wq_pk, L0_ffn_pk_keys, L0_ffn_Wq,
           L0_ffn_keys_table, L0_ffn_values_table, L0_ffn_Wo):
    import numpy as np
    import concourse.bacc as bacc
    from concourse.bass_utils import run_bass_kernel_spmd

    n, d = np.shape(x)
    tiles = -(-n // P)
    xp = np.zeros((tiles * P, d), np.asarray(x).dtype)
    xp[:n] = x
    xp = np.ascontiguousarray(xp.reshape(tiles, P, d).transpose(1, 0, 2))
    adjp = np.zeros((tiles * P, n), np.asarray(adj).dtype)
    adjp[:n] = adj
    a = np.asarray(L0_gnn_a)[:, 0]
    hd = a.shape[0] // 2
    gh = d // hd
    a_both = np.zeros((d, 2 * gh), a.dtype)
    for h in range(gh):
        a_both[h * hd:(h + 1) * hd, h] = a[:hd]
        a_both[h * hd:(h + 1) * hd, gh + h] = a[hd:]
    a_bcast = np.ascontiguousarray(np.broadcast_to(a_both.reshape(d, 2, gh)[:, :, :, None], (d, 2, gh, P)))
    adjt = np.zeros((tiles * P, tiles * P), adjp.dtype)
    adjt[:n, :n] = np.asarray(adj).T
    gamma = np.ascontiguousarray(np.broadcast_to(np.asarray(L0_gnn_gamma)[None, :], (P, d)))
    beta = np.ascontiguousarray(np.broadcast_to(np.asarray(L0_gnn_beta)[None, :], (P, d)))
    pk = np.asarray(L0_ffn_pk_keys)
    halves, nk, nh, dk = pk.shape
    pk_t = np.ascontiguousarray(pk.transpose(3, 2, 0, 1)).reshape(dk, nh * halves, nk)
    wqpk = np.asarray(L0_ffn_Wq_pk).reshape(d, halves, nh, dk)
    wqpk_t = np.ascontiguousarray(wqpk.transpose(3, 2, 1, 0)).reshape(dk, nh * halves, d)
    wq = np.asarray(L0_ffn_Wq).reshape(d, nh, d)
    kv = np.concatenate([np.asarray(L0_ffn_keys_table), np.asarray(L0_ffn_values_table)], axis=1)
    wo = np.ascontiguousarray(np.asarray(L0_ffn_Wo).reshape(nh, d, d).transpose(1, 0, 2))

    nc = bacc.Bacc("TRN2", target_bir_lowering=False, num_devices=1)
    arrays = {"x_rows": xp, "adj_rows": adjp, "adj_cols": adjt, "gnn_w": np.asarray(L0_gnn_W), "a_both": a_both, "a_bcast": a_bcast,
              "gamma": gamma, "beta": beta, "wqpk_t": wqpk_t, "pk_t": pk_t, "wq": wq, "kv_table": kv, "wo": wo}
    args = [nc.dram_tensor(name, v.shape, mybir.dt.from_np(v.dtype), kind="ExternalInput").ap()
            for name, v in arrays.items()]
    out = nc.dram_tensor("out_rows", (tiles * P, d), F32, kind="ExternalOutput").ap()
    build(nc, *args, out)
    r = run_bass_kernel_spmd(nc, [arrays], core_ids=[0])
    return r.results[0]["out_rows"][:n]
```
